# Optimizing a Trainium2 kernel written in Bass

```python
import numpy as np
import jax
import jax.numpy as jnp

def _softmax(x, axis=-1):
    return jax.nn.softmax(x, axis=axis)

def _gelu(x):
    return jax.nn.gelu(x, approximate=True)

def _silu(x):
    return jax.nn.silu(x)

def _sigmoid(x):
    return jax.nn.sigmoid(x)

def _layernorm(x, axis=-1, eps=1e-05):
    m = jnp.mean(x, axis=axis, keepdims=True)
    v = jnp.var(x, axis=axis, keepdims=True)
    return (x - m) / jnp.sqrt(v + eps)

def _scatter_add(tgt, idx, src, axis=0):
    return tgt.at[idx].add(src)

def _segment_sum(src, seg, n):
    return jax.ops.segment_sum(src, seg, n)
kernel_name = 'mk_hybrid_d2_jaxref_r8_4a0ee8'

def setup_inputs(seed: int=0):
    np.random.seed(seed)
    _w = jnp.asarray

    def _L0_attn_a_setup():
        import jax, jax.numpy as jnp
        import numpy as np
        B, S, D = (2, 256, 512)
        H = 32
        HD = D // H
        THETA = 10000.0

        def _rope_cos_sin(seq_len, head_dim, theta=THETA):
            inv = 1.0 / theta ** (np.arange(0, head_dim, 2)[:head_dim // 2].astype(np.float32) / head_dim)
            t = np.arange(seq_len)
            f = np.outer(t, inv).astype(np.float32)
            return (jnp.asarray(np.cos(f)), jnp.asarray(np.sin(f)))

        def _apply_rotary(x, cos, sin):
            xr = x.astype(jnp.float32).reshape(*x.shape[:-1], HD // 2, 2)
            x0, x1 = (xr[..., 0], xr[..., 1])
            c = cos[None, :, None, :]
            s = sin[None, :, None, :]
            o0 = x0 * c - x1 * s
            o1 = x0 * s + x1 * c
            return jnp.stack((o0, o1), axis=-1).reshape(*x.shape[:-1], HD)
        key = jax.random.key(seed)
        ks = jax.random.split(key, 5)
        std = 0.02
        return {'x': jax.random.normal(ks[0], (B, S, D), dtype=jnp.float32), 'wq': jax.random.normal(ks[1], (D, D), dtype=jnp.float32) * std, 'wk': jax.random.normal(ks[2], (D, D), dtype=jnp.float32) * std, 'wv': jax.random.normal(ks[3], (D, D), dtype=jnp.float32) * std, 'wo': jax.random.normal(ks[4], (D, D), dtype=jnp.float32) * std}
    _L0_attn_a_in = _L0_attn_a_setup()

    def _L0_attn_b_setup():
        import jax, jax.numpy as jnp
        import numpy as np
        D_MODEL = 512
        NUM_HEADS = 32
        HEAD_DIM = D_MODEL // NUM_HEADS
        Q_LAT = 12
        KV_LAT = 4
        B, S = (2, 256)
        key = jax.random.key(seed)
        ks = jax.random.split(key, 6)
        sc = lambda fan_in: 1.0 / np.sqrt(fan_in)
        return {'x': jax.random.normal(ks[0], (B, S, D_MODEL), jnp.float32), 'Wq_d': jax.random.normal(ks[1], (D_MODEL, Q_LAT), jnp.float32) * sc(D_MODEL), 'bq_d': jnp.zeros((Q_LAT,), jnp.float32), 'W_qk': jax.random.normal(ks[2], (Q_LAT, NUM_HEADS * KV_LAT), jnp.float32) * sc(Q_LAT), 'b_qk': jnp.zeros((NUM_HEADS * KV_LAT,), jnp.float32), 'Wkv_d': jax.random.normal(ks[3], (D_MODEL, KV_LAT), jnp.float32) * sc(D_MODEL), 'bkv_d': jnp.zeros((KV_LAT,), jnp.float32), 'Wv_u': jax.random.normal(ks[4], (KV_LAT, NUM_HEADS * HEAD_DIM), jnp.float32) * sc(KV_LAT), 'bv_u': jnp.zeros((NUM_HEADS * HEAD_DIM,), jnp.float32), 'Wo': jax.random.normal(ks[5], (NUM_HEADS * HEAD_DIM, D_MODEL), jnp.float32) * sc(NUM_HEADS * HEAD_DIM), 'bo': jnp.zeros((D_MODEL,), jnp.float32)}
    _L0_attn_b_in = _L0_attn_b_setup()

    def _L0_ffn_setup():
        import jax, jax.numpy as jnp
        import numpy as np
        HIDDEN = 512
        INTER = 1376
        RANK = 128
        B, S = (2, 256)
        key = jax.random.key(seed)
        ks = jax.random.split(key, 7)
        sc = 0.02
        return {'x': jax.random.normal(ks[0], (B, S, HIDDEN), dtype=jnp.float32), 'U1': jax.random.normal(ks[1], (HIDDEN, RANK), dtype=jnp.float32) * sc, 'V1': jax.random.normal(ks[2], (RANK, 2 * INTER), dtype=jnp.float32) * sc, 'U2': jax.random.normal(ks[3], (INTER, RANK), dtype=jnp.float32) * sc, 'V2': jax.random.normal(ks[4], (RANK, HIDDEN), dtype=jnp.float32) * sc, 'b1': jax.random.normal(ks[5], (2 * INTER,), dtype=jnp.float32) * sc, 'b2': jax.random.normal(ks[6], (HIDDEN,), dtype=jnp.float32) * sc}
    _L0_ffn_in = _L0_ffn_setup()

    def _L1_attn_a_setup():
        import jax, jax.numpy as jnp
        import numpy as np
        H = 512
        D_IN = 1024
        N = 16
        K = 4
        R = 32
        EPS = 1e-06

        def rms_forward(x, eps=EPS):
            xf = x.astype(jnp.float32)
            var = jnp.mean(xf * xf, axis=-1, keepdims=True)
            return (xf * jax.lax.rsqrt(var + eps)).astype(x.dtype)
        key = jax.random.key(seed)
        ks = jax.random.split(key, 10)
        s = 0.02
        hidden_states = jax.random.normal(ks[0], (2, 128, H), dtype=jnp.float32)
        W_in = jax.random.normal(ks[1], (2 * D_IN, H), dtype=jnp.float32) * s
        conv_w = jax.random.normal(ks[2], (D_IN, K), dtype=jnp.float32) * 0.2
        conv_b = jax.random.normal(ks[3], (D_IN,), dtype=jnp.float32) * 0.02
        W_x = jax.random.normal(ks[4], (R + 2 * N, D_IN), dtype=jnp.float32) * s
        W_dt = jax.random.normal(ks[5], (D_IN, R), dtype=jnp.float32) * s
        b_dt = jax.random.normal(ks[6], (D_IN,), dtype=jnp.float32) * 0.02
        A_log = jnp.log(jnp.broadcast_to(jnp.arange(1, N + 1, dtype=jnp.float32)[None, :], (D_IN, N)))
        D = jnp.ones((D_IN,), dtype=jnp.float32)
        W_out = jax.random.normal(ks[7], (H, D_IN), dtype=jnp.float32) * s
        return {'hidden_states': hidden_states, 'W_in': W_in, 'conv_w': conv_w, 'conv_b': conv_b, 'W_x': W_x, 'W_dt': W_dt, 'b_dt': b_dt, 'A_log': A_log, 'D': D, 'W_out': W_out}
    _L1_attn_a_in = _L1_attn_a_setup()

    def _L1_attn_b_setup():
        import jax, jax.numpy as jnp
        import numpy as np
        B, T, D = (1, 256, 512)
        H, G = (32, 8)
        HD = D // H
        REP = H // G
        KV_DIM = 2 * HD * G
        key = jax.random.key(seed)
        k0, k1, k2, k3 = jax.random.split(key, 4)
        x = jax.random.normal(k0, (B, T, D), dtype=jnp.float32)
        Wq = jax.random.normal(k1, (D, D), dtype=jnp.float32) * 0.02
        Wkv = jax.random.normal(k2, (D, KV_DIM), dtype=jnp.float32) * 0.02
        Wo = jax.random.normal(k3, (D, D), dtype=jnp.float32) * 0.02
        bo = jnp.zeros((D,), dtype=jnp.float32)
        return {'x': x, 'Wq': Wq, 'Wkv': Wkv, 'Wo': Wo, 'bo': bo}
    _L1_attn_b_in = _L1_attn_b_setup()

    def _L1_ffn_setup():
        import jax, jax.numpy as jnp
        import numpy as np
        NF4 = jnp.array([-1.0, -0.6961928009986877, -0.5250730514526367, -0.39491748809814453, -0.28444138169288635, -0.18477343022823334, -0.09105003625154495, 0.0, 0.07958029955625534, 0.16093020141124725, 0.24611230194568634, 0.33791524171829224, 0.44070982933044434, 0.5626170039176941, 0.7229568362236023, 1.0], dtype=jnp.float32)
        BLOCK = 64

        def _dequant_nf4(codes, absmax):
            vals = NF4[codes.reshape(-1)]
            w = vals.reshape(-1, BLOCK) * absmax[:, None]
            return w.reshape(codes.shape)
        key = jax.random.key(seed)
        k1, k2, k3, k4 = jax.random.split(key, 4)
        out_f, in_f = (512, 512)
        x = jax.random.normal(k1, (4, 256, in_f), dtype=jnp.float32)
        codes = jax.random.randint(k2, (out_f, in_f), 0, 16, dtype=jnp.int32)
        absmax = jax.random.uniform(k3, (out_f * in_f // BLOCK,), dtype=jnp.float32)
        bias = jax.random.normal(k4, (out_f,), dtype=jnp.float32)
        return {'x': x, 'codes': codes, 'absmax': absmax, 'bias': bias}
    _L1_ffn_in = _L1_ffn_setup()
    _d = {'L0_attn_a_x': _L0_attn_a_in['x'], 'L0_attn_a_wq': _L0_attn_a_in['wq'], 'L0_attn_a_wk': _L0_attn_a_in['wk'], 'L0_attn_a_wv': _L0_attn_a_in['wv'], 'L0_attn_a_wo': _L0_attn_a_in['wo'], 'L0_attn_b_Wq_d': _L0_attn_b_in['Wq_d'], 'L0_attn_b_bq_d': _L0_attn_b_in['bq_d'], 'L0_attn_b_W_qk': _L0_attn_b_in['W_qk'], 'L0_attn_b_b_qk': _L0_attn_b_in['b_qk'], 'L0_attn_b_Wkv_d': _L0_attn_b_in['Wkv_d'], 'L0_attn_b_bkv_d': _L0_attn_b_in['bkv_d'], 'L0_attn_b_Wv_u': _L0_attn_b_in['Wv_u'], 'L0_attn_b_bv_u': _L0_attn_b_in['bv_u'], 'L0_attn_b_Wo': _L0_attn_b_in['Wo'], 'L0_attn_b_bo': _L0_attn_b_in['bo'], 'L0_ffn_U1': _L0_ffn_in['U1'], 'L0_ffn_V1': _L0_ffn_in['V1'], 'L0_ffn_U2': _L0_ffn_in['U2'], 'L0_ffn_V2': _L0_ffn_in['V2'], 'L0_ffn_b1': _L0_ffn_in['b1'], 'L0_ffn_b2': _L0_ffn_in['b2'], 'L1_attn_a_W_in': _L1_attn_a_in['W_in'], 'L1_attn_a_conv_w': _L1_attn_a_in['conv_w'], 'L1_attn_a_conv_b': _L1_attn_a_in['conv_b'], 'L1_attn_a_W_x': _L1_attn_a_in['W_x'], 'L1_attn_a_W_dt': _L1_attn_a_in['W_dt'], 'L1_attn_a_b_dt': _L1_attn_a_in['b_dt'], 'L1_attn_a_A_log': _L1_attn_a_in['A_log'], 'L1_attn_a_D': _L1_attn_a_in['D'], 'L1_attn_a_W_out': _L1_attn_a_in['W_out'], 'L1_attn_b_Wq': _L1_attn_b_in['Wq'], 'L1_attn_b_Wkv': _L1_attn_b_in['Wkv'], 'L1_attn_b_Wo': _L1_attn_b_in['Wo'], 'L1_attn_b_bo': _L1_attn_b_in['bo'], 'L1_ffn_codes': _L1_ffn_in['codes'], 'L1_ffn_absmax': _L1_ffn_in['absmax'], 'L1_ffn_bias': _L1_ffn_in['bias']}
    _x0 = _d['L0_attn_a_x']
    _d['L0_attn_a_x'] = jax.random.normal(jax.random.fold_in(jax.random.key(seed), 1), (4, 512, 512), dtype=_x0.dtype)
    del _x0
    return _d

def reference(L0_attn_a_x, L0_attn_a_wq, L0_attn_a_wk, L0_attn_a_wv, L0_attn_a_wo, L0_attn_b_Wq_d, L0_attn_b_bq_d, L0_attn_b_W_qk, L0_attn_b_b_qk, L0_attn_b_Wkv_d, L0_attn_b_bkv_d, L0_attn_b_Wv_u, L0_attn_b_bv_u, L0_attn_b_Wo, L0_attn_b_bo, L0_ffn_U1, L0_ffn_V1, L0_ffn_U2, L0_ffn_V2, L0_ffn_b1, L0_ffn_b2, L1_attn_a_W_in, L1_attn_a_conv_w, L1_attn_a_conv_b, L1_attn_a_W_x, L1_attn_a_W_dt, L1_attn_a_b_dt, L1_attn_a_A_log, L1_attn_a_D, L1_attn_a_W_out, L1_attn_b_Wq, L1_attn_b_Wkv, L1_attn_b_Wo, L1_attn_b_bo, L1_ffn_codes, L1_ffn_absmax, L1_ffn_bias):

    def _L0_attn_a_ref(x, wq, wk, wv, wo):
        import jax, jax.numpy as jnp
        import numpy as np
        B, S, D = (2, 256, 512)
        H = 32
        HD = D // H
        THETA = 10000.0

        def _rope_cos_sin(seq_len, head_dim, theta=THETA):
            inv = 1.0 / theta ** (np.arange(0, head_dim, 2)[:head_dim // 2].astype(np.float32) / head_dim)
            t = np.arange(seq_len)
            f = np.outer(t, inv).astype(np.float32)
            return (jnp.asarray(np.cos(f)), jnp.asarray(np.sin(f)))

        def _apply_rotary(x, cos, sin):
            xr = x.astype(jnp.float32).reshape(*x.shape[:-1], HD // 2, 2)
            x0, x1 = (xr[..., 0], xr[..., 1])
            c = cos[None, :, None, :]
            s = sin[None, :, None, :]
            o0 = x0 * c - x1 * s
            o1 = x0 * s + x1 * c
            return jnp.stack((o0, o1), axis=-1).reshape(*x.shape[:-1], HD)
        b, s, d = x.shape
        q = (x @ wq).reshape(b, s, H, HD)
        k = (x @ wk).reshape(b, s, H, HD)
        v = (x @ wv).reshape(b, s, H, HD)
        cos, sin = _rope_cos_sin(s, HD)
        q = _apply_rotary(q, cos, sin)
        k = _apply_rotary(k, cos, sin)
        scale = 1.0 / jnp.sqrt(jnp.float32(HD))
        scores = jnp.einsum('bqhd,bkhd->bhqk', q, k) * scale
        causal = jnp.tril(jnp.ones((s, s), dtype=bool))
        scores = jnp.where(causal[None, None], scores, jnp.finfo(scores.dtype).min)
        probs = jax.nn.softmax(scores, axis=-1)
        out = jnp.einsum('bhqk,bkhd->bqhd', probs, v).reshape(b, s, d)
        return out @ wo

    def _L0_attn_b_ref(x, Wq_d, bq_d, W_qk, b_qk, Wkv_d, bkv_d, Wv_u, bv_u, Wo, bo):
        import jax, jax.numpy as jnp
        import numpy as np
        D_MODEL = 512
        NUM_HEADS = 32
        HEAD_DIM = D_MODEL // NUM_HEADS
        Q_LAT = 12
        KV_LAT = 4
        B, S = (2, 256)
        b, s, _ = x.shape
        C_q = x @ Wq_d + bq_d
        C_kv = x @ Wkv_d + bkv_d
        q = (C_q @ W_qk + b_qk).reshape(b, s, NUM_HEADS, KV_LAT)
        scores = jnp.einsum('bqhd,bkd->bhqk', q, C_kv) / jnp.sqrt(jnp.asarray(KV_LAT, x.dtype))
        attn = jax.nn.softmax(scores, axis=-1)
        V = (C_kv @ Wv_u + bv_u).reshape(b, s, NUM_HEADS, HEAD_DIM)
        out = jnp.einsum('bhqk,bkhd->bqhd', attn, V).reshape(b, s, NUM_HEADS * HEAD_DIM)
        return out @ Wo + bo

    def _L0_ffn_ref(x, U1, V1, U2, V2, b1, b2):
        import jax, jax.numpy as jnp
        import numpy as np
        HIDDEN = 512
        INTER = 1376
        RANK = 128
        B, S = (2, 256)
        P = jnp.einsum('bsh,hr->bsr', x, U1)
        H = jnp.einsum('bsr,rf->bsf', P, V1) + b1
        gate, up = (H[..., :INTER], H[..., INTER:])
        act = jax.nn.silu(gate) * up
        Z = jnp.einsum('bsi,ir->bsr', act, U2)
        out = jnp.einsum('bsr,rh->bsh', Z, V2) + b2
        return out

    def _L1_attn_a_ref(hidden_states, W_in, conv_w, conv_b, W_x, W_dt, b_dt, A_log, D, W_out):
        import jax, jax.numpy as jnp
        import numpy as np
        H = 512
        D_IN = 1024
        N = 16
        K = 4
        R = 32
        EPS = 1e-06

        def rms_forward(x, eps=EPS):
            xf = x.astype(jnp.float32)
            var = jnp.mean(xf * xf, axis=-1, keepdims=True)
            return (xf * jax.lax.rsqrt(var + eps)).astype(x.dtype)
        b, L, _ = hidden_states.shape
        proj = hidden_states @ W_in.T
        x, gate = (proj[..., :D_IN], proj[..., D_IN:])
        xpad = jnp.pad(x, ((0, 0), (K - 1, 0), (0, 0)))
        xc = conv_b
        for j in range(K):
            xc = xc + conv_w[:, j] * xpad[:, j:j + L, :]
        x = jax.nn.silu(xc)
        ssm = x @ W_x.T
        ts, Bm, Cm = (ssm[..., :R], ssm[..., R:R + N], ssm[..., R + N:])
        ts = rms_forward(ts)
        Bm = rms_forward(Bm)
        Cm = rms_forward(Cm)
        dt = jax.nn.softplus(ts @ W_dt.T + b_dt)
        A = -jnp.exp(A_log.astype(jnp.float32))

        def step(state, inp):
            dt_t, B_t, C_t, u_t = inp
            dA = jnp.exp(dt_t[..., None] * A)
            state = state * dA + (dt_t * u_t)[..., None] * B_t[:, None, :]
            y = jnp.einsum('bdn,bn->bd', state, C_t)
            return (state, y)
        init = jnp.zeros((b, D_IN, N), dtype=jnp.float32)
        xs = (dt.transpose(1, 0, 2), Bm.transpose(1, 0, 2), Cm.transpose(1, 0, 2), x.transpose(1, 0, 2))
        _, ys = jax.lax.scan(step, init, xs)
        y = ys.transpose(1, 0, 2) + x * D
        y = y * jax.nn.silu(gate)
        return y @ W_out.T

    def _L1_attn_b_ref(x, Wq, Wkv, Wo, bo):
        import jax, jax.numpy as jnp
        import numpy as np
        B, T, D = (1, 256, 512)
        H, G = (32, 8)
        HD = D // H
        REP = H // G
        KV_DIM = 2 * HD * G
        b, t, d = x.shape
        q = jnp.dot(x, Wq).reshape(b, t, H, HD).transpose(0, 2, 1, 3)
        kv = jnp.dot(x, Wkv).reshape(b, t, G, 2, HD).transpose(2, 3, 0, 1, 4)
        k, v = (kv[:, 0], kv[:, 1])
        k = jnp.broadcast_to(k[:, :, None], (G, b, REP, t, HD)).reshape(b, H, t, HD)
        v = jnp.broadcast_to(v[:, :, None], (G, b, REP, t, HD)).reshape(b, H, t, HD)
        scores = jnp.einsum('bhqd,bhkd->bhqk', q, k)
        causal = jnp.triu(jnp.ones((t, t), dtype=bool), 1)
        scores = jnp.where(causal[None, None], -jnp.inf, scores)
        weights = jax.nn.softmax(scores * (1.0 / HD ** 0.5), axis=-1)
        ctx = jnp.einsum('bhqk,bhkd->bhqd', weights, v)
        ctx = ctx.transpose(0, 2, 1, 3).reshape(b, t, d)
        return jnp.dot(ctx, Wo) + bo

    def _L1_ffn_ref(x, codes, absmax, bias):
        import jax, jax.numpy as jnp
        import numpy as np
        NF4 = jnp.array([-1.0, -0.6961928009986877, -0.5250730514526367, -0.39491748809814453, -0.28444138169288635, -0.18477343022823334, -0.09105003625154495, 0.0, 0.07958029955625534, 0.16093020141124725, 0.24611230194568634, 0.33791524171829224, 0.44070982933044434, 0.5626170039176941, 0.7229568362236023, 1.0], dtype=jnp.float32)
        BLOCK = 64

        def _dequant_nf4(codes, absmax):
            vals = NF4[codes.reshape(-1)]
            w = vals.reshape(-1, BLOCK) * absmax[:, None]
            return w.reshape(codes.shape)
        w = _dequant_nf4(codes, absmax)
        out = jnp.einsum('bsd,od->bso', x, w)
        return out + bias
    x = L0_attn_a_x
    x = x + _L0_attn_a_ref(_layernorm(x, axis=-1), L0_attn_a_wq, L0_attn_a_wk, L0_attn_a_wv, L0_attn_a_wo)
    x = x + _L0_ffn_ref(_layernorm(x, axis=-1), L0_ffn_U1, L0_ffn_V1, L0_ffn_U2, L0_ffn_V2, L0_ffn_b1, L0_ffn_b2)
    x = x + _L0_attn_b_ref(_layernorm(x, axis=-1), L0_attn_b_Wq_d, L0_attn_b_bq_d, L0_attn_b_W_qk, L0_attn_b_b_qk, L0_attn_b_Wkv_d, L0_attn_b_bkv_d, L0_attn_b_Wv_u, L0_attn_b_bv_u, L0_attn_b_Wo, L0_attn_b_bo)
    x = x + _L0_ffn_ref(_layernorm(x, axis=-1), L0_ffn_U1, L0_ffn_V1, L0_ffn_U2, L0_ffn_V2, L0_ffn_b1, L0_ffn_b2)
    x = x + _L1_attn_a_ref(_layernorm(x, axis=-1), L1_attn_a_W_in, L1_attn_a_conv_w, L1_attn_a_conv_b, L1_attn_a_W_x, L1_attn_a_W_dt, L1_attn_a_b_dt, L1_attn_a_A_log, L1_attn_a_D, L1_attn_a_W_out)
    x = x + _L1_ffn_ref(_layernorm(x, axis=-1), L1_ffn_codes, L1_ffn_absmax, L1_ffn_bias)
    x = x + _L1_attn_b_ref(_layernorm(x, axis=-1), L1_attn_b_Wq, L1_attn_b_Wkv, L1_attn_b_Wo, L1_attn_b_bo)
    x = x + _L1_ffn_ref(_layernorm(x, axis=-1), L1_ffn_codes, L1_ffn_absmax, L1_ffn_bias)
    return x

_drawn_inputs = setup_inputs


def setup_inputs(seed=0):
    import zlib

    import numpy as np

    out = dict(_drawn_inputs(seed))
    spreads = {'L0_attn_b_bq_d': (0.0, 0.8),
     'L0_attn_b_b_qk': (0.0, 0.8),
     'L0_attn_b_bkv_d': (0.0, 0.8),
     'L0_attn_b_bv_u': (0.0, 2.0),
     'L0_attn_b_bo': (0.0, 2.0),
     'L1_attn_a_D': (1.0, 0.6),
     'L1_attn_b_bo': (0.0, 2.0)}
    factors = {'L0_attn_a_wq': 8.0,
     'L0_attn_a_wk': 8.0,
     'L0_ffn_U1': 8.0,
     'L0_ffn_V1': 8.0,
     'L0_ffn_U2': 8.0,
     'L0_ffn_V2': 8.0,
     'L0_ffn_b1': 8.0,
     'L1_attn_a_conv_b': 58.824,
     'L1_attn_a_W_dt': 64.0,
     'L1_attn_a_b_dt': 64.0,
     'L1_attn_a_A_log': 58.096,
     'L1_attn_b_Wq': 64.0,
     'L1_attn_b_Wkv': 64.0,
     'L1_attn_b_Wo': 64.0,
     'L0_attn_b_Wq_d': 8.0,
     'L0_attn_b_W_qk': 8.0,
     'L0_attn_b_Wkv_d': 8.0,
     'L0_attn_b_Wv_u': 8.0,
     'L0_attn_b_Wo': 8.0,
     'L0_ffn_b2': 44.74,
     'L1_attn_a_W_in': 8.0,
     'L1_attn_a_conv_w': 8.0,
     'L1_attn_a_W_x': 8.0,
     'L1_attn_a_W_out': 8.0,
     'L1_ffn_absmax': 19.585,
     'L1_ffn_bias': 64.0}
    for name, (base, spread) in spreads.items():
        noise = np.random.default_rng([zlib.crc32(name.encode()), seed]).standard_normal(out[name].shape)
        drawn = base * np.exp(spread * noise) if base else spread * noise
        out[name] = jnp.asarray(drawn.astype(out[name].dtype))
    for name, factor in factors.items():
        out[name] = (out[name] * factor).astype(out[name].dtype)
    return out
```

```python
from contextlib import ExitStack

import concourse.bass as bass
from concourse import mybir

F32 = mybir.dt.float32
BF16 = mybir.dt.bfloat16
I32 = mybir.dt.int32
ALU = mybir.AluOpType
ACT = mybir.ActivationFunctionType
AX = mybir.AxisListType

P = 128
B, S, D = 4, 512, 512
NT = S // P
NC = D // P
H, HD = 32, 16
GRP = 4
NG = H // GRP
KVH = 8
LAT, QLAT = 4, 12
INTER, RANK = 1376, 128
NF = -(-INTER // P)
DI, NS, RDT = 1024, 16, 32
NM = DI // P
EPS_LN, EPS_RMS = 1e-5, 1e-6
MASKED = -1e30
NF4 = [-1.0, -0.6961928009986877, -0.5250730514526367, -0.39491748809814453, -0.28444138169288635,
       -0.18477343022823334, -0.09105003625154495, 0.0, 0.07958029955625534, 0.16093020141124725,
       0.24611230194568634, 0.33791524171829224, 0.44070982933044434, 0.5626170039176941,
       0.7229568362236023, 1.0]
LN_A, LN_F1, LN_M, LN_F2, LN_S, LN_N1, LN_KV = range(7)
LN_G, LN_N2 = range(2)


class Memory:

    def __init__(self, nc, ctx):
        def sb(name, shape, dt=F32):
            return ctx.enter_context(nc.sbuf_tensor(name, shape, dt))

        self.bank = ctx.enter_context(nc.psum_tensor("banks", [P, 8, 512], F32))
        self.bankb = self.bank[:, :, :].bitcast(BF16)
        self.x = sb("x_res", [P, NT, D])
        self.xT = sb("xT", [P, NC, S])
        self.xn = sb("xn", [P, 2, D])
        self.stats = sb("ln_stats", [P, NT, 6])
        self.mv = sb("ln_mean_var", [P, NT, 2])
        self.rstd = sb("ln_rstd", [P, NT])
        self.minus_half = sb("minus_half", [P, 16])
        self.ident = sb("ident", [P, P])
        self.identb = sb("identb", [P, P], BF16)
        self.maskS = sb("maskS", [P, P], BF16)
        self.maskT = sb("maskT", [P, P], BF16)
        self.cos = sb("cos", [P, NT, HD])
        self.sin = sb("sin", [P, NT, HD])
        self.nf4w = sb("nf4w", [P, NC, D])
        self.bias = sb("bias_rows", [P, 4, D])
        self.U1 = sb("U1", [P, NC, RANK])
        self.V1 = sb("V1", [P, 2 * INTER])
        self.U2 = sb("U2", [P, NF, RANK])
        self.V2 = sb("V2", [P, D])
        self.b1 = sb("b1", [P, 2, NF])
        self.wlat = sb("wlat", [P, NC, QLAT + LAT])
        self.blat = sb("blat", [P, QLAT + LAT])
        self.wqk = sb("wqk", [QLAT, H * LAT])
        self.bqk = sb("bqk", [P, H * LAT])
        self.wcomb = sb("wcomb", [P, D])
        self.convw = sb("convw", [P, NM, 4])
        self.convb = sb("convb", [P, NM])
        self.bdt = sb("bdt", [P, NM])
        self.Dskip = sb("Dskip", [P, NM])
        self.A = sb("A", [P, NM, NS])
        self.mx = sb("row_max", [P, 2, 16])
        self.mr = sb("max_rest", [P, 2, 16])
        self.mp = sb("max_parts", [P, 2, NT, 3 * GRP], BF16)
        self.mT = sb("max_rows", [3 * GRP, 2, S], BF16)
        self.recip = sb("recip", [P, 16])
        words = 35456
        self.arena = sb("arena", [P, words])
        a = self.view
        self.wA = a(0, 4 * NC * D).rearrange("p (w c n) -> p w c n", w=4, c=NC)
        self.qA = a(8192, H * S // 2).bitcast(BF16).rearrange("p (h s) -> p h s", h=H)
        self.kA = a(16384, H * S // 2).bitcast(BF16).rearrange("p (h s) -> p h s", h=H)
        self.tqA = a(24576, H * 50).bitcast(BF16).rearrange("p (h e) -> p h e", h=H)
        self.tkA = a(26176, H * 50).bitcast(BF16).rearrange("p (h e) -> p h e", h=H)
        self.vA = a(27776, NT * H * 32).rearrange("p (t h e) -> p t h e", t=NT, h=H)
        self.ra = a(31872, 512)
        self.rb = a(32384, 512)
        self.rqA = a(32896, 1024).rearrange("p (s n) -> p s n", s=2)
        self.rrA = a(34944, 512)
        self.oA = a(0, NT * D).rearrange("p (t n) -> p t n", t=NT)
        self.ostA = a(31872, 1024).rearrange("p (s n) -> p s n", s=2)
        self.probsA = a(2048, 8 * 512).rearrange("p (s n) -> p s n", s=8)
        self.nf_codes = [a(20480 + 512 * c, 512).bitcast(I32) for c in range(NC)]
        self.nf_absmax = [a(22528 + 512 * c, 512) for c in range(NC)]
        self.nf_tmps = [a(24576 + 512 * c, 512) for c in range(2)]
        self.qG = self.qA
        self.kG = a(16384, KVH * S // 2).bitcast(BF16).rearrange("p (h s) -> p h s", h=KVH)
        self.vG = a(18432, NT * KVH * 32).rearrange("p (t h e) -> p t h e", t=NT, h=KVH)
        self.tqG = a(19456, H * 50).bitcast(BF16).rearrange("p (h e) -> p h e", h=H)
        self.tkG = a(21056, KVH * 50).bitcast(BF16).rearrange("p (h e) -> p h e", h=KVH)
        self.probsG = a(21504, 8 * 512).rearrange("p (s n) -> p s n", s=8)
        self.oG = a(25600, NT * D).rearrange("p (t n) -> p t n", t=NT)
        self.ostG = a(27648, 1024).rearrange("p (s n) -> p s n", s=2)
        self.rqG = a(28672, 1024).rearrange("p (s n) -> p s n", s=2)
        self.rrG = a(29696, 512)
        self.wG = a(30208, 5120)
        self.kt = a(0, NT * P).rearrange("p (t n) -> p t n", t=NT)
        self.kvo = a(0, NT * 256).rearrange("p (t n) -> p t n", t=NT)
        self.pT = a(22016, 512)
        self.sg = a(22528, 2 * 512).rearrange("p (s n) -> p s n", s=2)
        self.act = a(23552, 3 * 512).rearrange("p (s n) -> p s n", s=3)
        self.zT = a(25088, 512)
        self.lat = a(22016, NT * 16).rearrange("p (t e) -> p t e", t=NT)
        self.cqT = a(22080, 512)
        self.qM = a(22592, NG * S // 2).bitcast(BF16).rearrange("p (h s) -> p h s", h=NG)
        self.kM = a(32384, 4 * S // 2).bitcast(BF16).rearrange("p (g s) -> p g s", g=GRP)
        self.tqM = a(24896, H * 16).bitcast(BF16).rearrange("p (h e) -> p h e", h=H)
        self.tkM = a(25408, NT * 4 * 16).bitcast(BF16).rearrange("p (t r e) -> p t r e", t=NT, r=4)
        self.vM = a(25664, NT * 32).rearrange("p (t e) -> p t e", t=NT)
        self.probsM = a(25792, 8 * 512).rearrange("p (s n) -> p s n", s=8)
        self.oM = a(29888, NT * P).rearrange("p (t n) -> p t n", t=NT)
        self.ostM = a(30400, 1024).rearrange("p (s n) -> p s n", s=2)
        self.rqM = a(31424, 256).rearrange("p (s n) -> p s n", s=2)
        self.rrM = a(31680, 128)
        self.oMT = a(31808, 512)
        self.kr = a(32320, NT * LAT).rearrange("p (t e) -> p t e", t=NT)
        self.kp = a(32336, 3 * NT * LAT // 2).bitcast(BF16).rearrange("p (r t e) -> p r t e", r=3, t=NT)
        self.win = a(8192, NC * 2 * DI).rearrange("p (z c n) -> p z c n", z=2, c=NC)
        self.brep = a(8192, 8 * 512).rearrange("p (n s) -> p n s", n=8)
        self.crep = a(12288, 8 * 512).rearrange("p (n s) -> p n s", n=8)
        self.wout = a(16384, NM * D).rearrange("p (m n) -> p m n", m=NM)
        self.wx = a(20480, NM * 64).rearrange("p (m n) -> p m n", m=NM)
        self.wdt = a(20992, DI)
        self.xs = a(22016, NM * S).rearrange("p (m s) -> p m s", m=NM)
        self.gate = a(26112, NM * S).rearrange("p (m s) -> p m s", m=NM)
        self.dt = a(30208, NM * S).rearrange("p (m s) -> p m s", m=NM)
        self.zdt = a(0, NM * S).rearrange("p (m s) -> p m s", m=NM)
        self.decay = a(0, 2 * 1024).rearrange("p (s j n) -> p s j n", s=2, j=2)
        self.drive = a(2048, 2 * 1024).rearrange("p (s j n) -> p s j n", s=2, j=2)
        self.state = a(4096, 2 * 1024).rearrange("p (s j n) -> p s j n", s=2, j=2)
        self.ssm = a(4096, NT * 64).rearrange("p (t e) -> p t e", t=NT)
        self.ssq = a(4352, NT * 64).rearrange("p (t e) -> p t e", t=NT)
        self.rms = a(4608, NT * 4).rearrange("p (t e) -> p t e", t=NT)
        self.ssmT = a(4624, 512)
        self.conv = a(6144, 2 * 512).rearrange("p (s n) -> p s n", s=2)
        self.yhi = a(6144, 4 * 512).rearrange("p (m n) -> p m n", m=4)
        self.bd = a(16384, NC * 32).rearrange("p (c n) -> p c n", c=NC)
        self.wo_lat = a(16512, NC * D).rearrange("p (c n) -> p c n", c=NC)
        self.bv = a(18560, NC)
        self.bvb = a(18564, NC * P).rearrange("p (c n) -> p c n", c=NC)
        self.bo_row = a(19076, D)
        self.alog = a(19588, NM * NS).rearrange("p (m n) -> p m n", m=NM)

    def view(self, at, words):
        return self.arena[:, at:at + words]

    def plus(self, m):
        return self.brep[:, m, :]

    def y(self, m):
        return self.xT[:, m, :] if m < NC else self.yhi[:, m - NC, :]


class Signals:

    def __init__(self, once, each):
        self.n_consts = 16 * 22
        sem = once
        self.ident_made = sem("ident_made")
        self.masks_cleared = sem("masks_cleared")
        self.bd_cleared = sem("bd_cleared")
        self.consts_loaded = sem("consts_loaded")
        self.latent_loaded = sem("latent_loaded")
        self.bvb_made = sem("bvb_made")
        self.wcomb_made = sem("wcomb_made")
        self.wcomb_copied = sem("wcomb_copied")
        self.latent_bias = sem("latent_bias")
        self.bias_made = sem("bias_made")
        self.a_exp = sem("a_exp")
        self.alog_held = sem("alog_held")
        self.nf4_ready = sem("nf4_ready")
        self.gqa_w_loaded = sem("gqa_w_loaded")
        self.codes_loaded = [sem(f"codes_loaded_{n}") for n in range(NC)]
        self.nf_steps = [sem(f"nf_steps_{n}") for n in range(NC)]
        sem = each
        self.x_loaded = sem("x_loaded")
        self.x_updated = sem("x_updated")
        self.biased = sem("biased")
        self.ln_stats = sem("ln_stats")
        self.ln_aggr = sem("ln_aggr")
        self.ln_eps = sem("ln_eps")
        self.ln_rstd = sem("ln_rstd")
        self.ln_xn = sem("ln_xn")
        self.ln_turned = sem("ln_turned")
        self.ln_copied = sem("ln_copied")
        self.lat_made = sem("lat_made")
        self.lat_ready = sem("lat_ready")
        self.cq_turned = sem("cq_turned")
        self.cq_copied = sem("cq_copied")
        self.klat_stacked = sem("klat_stacked")
        self.klat_turned = sem("klat_turned")
        self.klat_placed = sem("klat_placed")
        self.vlat_made = sem("vlat_made")
        self.n1_made = sem("n1_made")
        self.n2_made = sem("n2_made")
        self.win_loaded = sem("win_loaded")
        self.wx_loaded = sem("wx_loaded")
        self.wout_loaded = sem("wout_loaded")
        self.inner_made = sem("inner_made")
        self.convolved = sem("convolved")
        self.xs_made = sem("xs_made")
        self.gates = sem("gates")
        self.ssm_made = sem("ssm_made")
        self.ssm_steps = sem("ssm_steps")
        self.ssm_squares = sem("ssm_squares")
        self.rms_steps = sem("rms_steps")
        self.ssm_normed = sem("ssm_normed")
        self.ssm_turned = sem("ssm_turned")
        self.ssm_copied = sem("ssm_copied")
        self.z_made = sem("z_made")
        self.z_read = sem("z_read")
        self.dt_steps = sem("dt_steps")
        self.one_added = sem("one_added")
        self.one_plus = sem("one_plus")
        self.log_made = sem("log_made")
        self.logs = sem("logs")
        self.dt_made = sem("dt_made")
        self.decay_cleared = sem("decay_cleared")
        self.decays = sem("decays")
        self.du_made = sem("du_made")
        self.driven = sem("driven")
        self.scanned = sem("scanned")
        self.weighted = sem("weighted")
        self.summed = sem("summed")
        self.skipped = sem("skipped")
        self.y_kept = sem("y_kept")
        self.y_made = sem("y_made")
        self.scan_out_made = sem("scan_out_made")
        self.rows_stored = sem("rows_stored")
        self.wkv_loaded = sem("wkv_loaded")
        self.kv_made = sem("kv_made")
        self.kv_copied = sem("kv_copied")
        self.stored = sem("stored")
        self.lap = sem("lap")
        self.rep_b = [sem(f"rep_b_{k}") for k in range(4)]
        self.rep_c = [sem(f"rep_c_{k}") for k in range(4)]



def ln_vector(dve, m, s, i):
    for t in range(NT):
        if i == 0:
            dve.wait_ge(s.x_loaded, 16)
        else:
            dve.wait_ge(s.x_updated, NT * (i - 1) + t + 1)
        dve.bn_stats(m.stats[:, t, :], m.x[:, t, :]).then_inc(s.ln_stats, 1)
        dve.wait_ge(s.ln_stats, NT * i + t + 1)
        dve.bn_aggr(m.mv[:, t, :], m.stats[:, t, :]).then_inc(s.ln_aggr, 1)
    for t in range(NT):
        n = NT * i + t
        dve.wait_ge(s.ln_rstd, n + 1)
        if n >= 2:
            dve.wait_ge(s.ln_turned, n - 1)
        dve.tensor_scalar(m.xn[:, t % 2, :], m.x[:, t, :], m.mv[:, t, 0:1], m.rstd[:, t:t + 1],
                          ALU.subtract, ALU.mult).then_inc(s.ln_xn, 1)


def ln_gpsimd(pool, m, s, i):
    for t in range(NT):
        n = NT * i + t
        pool.wait_ge(s.ln_aggr, n + 1)
        pool.tensor_scalar(m.rstd[:, t:t + 1], m.mv[:, t, 1:2], EPS_LN, None, ALU.add).then_inc(s.ln_eps, 1)
        pool.wait_ge(s.ln_eps, n + 1)
        pool.tensor_tensor(m.rstd[:, t:t + 1], m.rstd[:, t:t + 1], m.minus_half[:, 0:1],
                           ALU.pow).then_inc(s.ln_rstd, 1)


def ln_tensor(pe, m, s, i):
    for t in range(NT):
        n = NT * i + t
        pe.wait_ge(s.ln_xn, n + 1)
        if n >= 2:
            pe.wait_ge(s.ln_copied, n - 1)
        for c in range(NC):
            mm = pe.transpose(m.bank[:, 6 + t % 2, c * P:(c + 1) * P],
                              m.xn[:, t % 2, c * P:(c + 1) * P], m.ident[:, :])
        mm.then_inc(s.ln_turned, 1)


def ln_scalar(act, m, s, i):
    for t in range(NT):
        act.wait_ge(s.ln_turned, NT * i + t + 1)
        act.activation(m.xT[:, :, t * P:(t + 1) * P],
                       m.bank[:, 6 + t % 2, :].rearrange("p (c n) -> p c n", c=NC),
                       ACT.Copy).then_inc(s.ln_copied, 1)


def add_bias_gpsimd(pool, m, s, i, k, row):
    for t in range(NT):
        pool.wait_ge(s.ln_xn, NT * i + t + 1)
        pool.tensor_tensor(m.x[:, t, :], m.x[:, t, :], m.bias[:, row, :], ALU.add).then_inc(s.biased, 1)


def residual_vector(dve, m, s, i, made, bank, k=None):
    for t in range(NT):
        dve.wait_ge(made, t + 1)
        if k is not None:
            dve.wait_ge(s.biased, NT * k + t + 1)
        dve.tensor_tensor(m.x[:, t, :], m.x[:, t, :], m.bank[:, bank(t), :],
                          ALU.add).then_inc(s.x_updated, 1)


class Attention:

    def __init__(self, sem, i, causal, scale, vdim, q, k, v, probs, o, ost, kv_heads=H):
        self.projected = sem("att_projected")
        self.rope_a = sem("att_rope_a")
        self.rope_b = sem("att_rope_b")
        self.rotated = sem("att_rotated")
        self.split1 = sem("att_split1")
        self.rest = sem("att_rest")
        self.split2 = sem("att_split2")
        self.stacked = sem("att_stacked")
        self.turned = sem("att_turned")
        self.placed_dve = sem("att_placed_dve")
        self.placed_act = sem("att_placed_act")
        self.v_read = sem("att_v_read")
        self.consts = sem("att_consts")
        self.scored = sem("att_scored")
        self.maxed = sem("att_maxed")
        self.m_parts = sem("att_m_parts")
        self.m_rest = sem("att_m_rest")
        self.m_turned = sem("att_m_turned")
        self.m_copied = sem("att_m_copied")
        self.m_placed = sem("att_m_placed")
        self.shifted = sem("att_shifted")
        self.exped = sem("att_exped")
        self.valued = sem("att_valued")
        self.o_copied = sem("att_o_copied")
        self.o_turned = sem("att_o_turned")
        self.recips = sem("att_recips")
        self.normed = sem("att_normed")
        self.out_turned = sem("att_out_turned")
        self.out_copied = sem("att_out_copied")
        self.out_made = sem("att_out_made")
        self.w_loaded = sem("att_w_loaded")
        self.kv_loaded = sem("att_kv_loaded")
        self.i, self.causal, self.scale, self.vdim = i, causal, scale, vdim
        self.q, self.k, self.v = q, k, v
        self.probs, self.o, self.ost, self.kv_heads = probs, o, ost, kv_heads
        self.rope = kv_heads == H


def width_s(a, qt):
    return P * (qt + 1) if a.causal else S


def first_t(a, kt):
    return P * kt if a.causal else 0


AHEAD = 28
TURN_AT, COPY_AT = 3, 4
UNITS = NG * NT * GRP


def max_unit(u):
    hg, v = divmod(u, NT * GRP)
    return hg, (v // GRP - AHEAD // GRP) % NT, v % GRP


def attend_tensor(pe, m, a, stacks_ready):
    def scores(u):
        hg, qt, g = max_unit(u)
        w = width_s(a, qt)
        if u >= 2:
            pe.wait_ge(a.maxed, u - 1)
        out = m.bank[:, u % 2, 0:w]
        mm = pe.matmul(out, a.q(GRP * hg + g)[:, qt * P:(qt + 1) * P], a.k(GRP * hg + g)[:, 0:w],
                       start=True, stop=not a.causal)
        if a.causal:
            mm = pe.matmul(m.bank[:, u % 2, w - P:w], m.identb[:, :], m.maskS[:, :], start=False, stop=True)
        mm.then_inc(a.scored, 1)

    def turn_maxima(hg):
        pe.wait_ge(a.m_parts, 3 * (hg + 1))
        if hg >= 1:
            pe.wait_ge(a.m_copied, hg)
        for qt in range(NT):
            mm = pe.transpose(m.bankb[0:3 * GRP, 6, qt * P:(qt + 1) * P], m.mp[:, hg % 2, qt, :],
                              m.identb[:, :])
        mm.then_inc(a.m_turned, 1)

    def shifted_scores(hg, v):
        kt, g = divmod(v, GRP)
        u, lo = 16 * hg + v, first_t(a, kt)
        if v == 0:
            pe.wait_ge(a.m_placed, 48 * (hg + 1))
        if u >= 3:
            pe.wait_ge(a.exped, u - 2)
        w = S - lo
        mm = pe.matmul(m.bank[:, 2 + u % 3, 0:w], a.k(GRP * hg + g)[:, kt * P:(kt + 1) * P],
                       a.q(GRP * hg + g)[:, lo:S], start=True, stop=not a.causal)
        if a.causal:
            mm = pe.matmul(m.bank[:, 2 + u % 3, 0:P], m.identb[:, :], m.maskT[:, :], start=False, stop=True)
        mm.then_inc(a.shifted, 1)

    def values(n):
        hg, kt = divmod(n, NT)
        lo = first_t(a, kt)
        pe.wait_ge(a.exped, GRP * (n + 1))
        if kt == 0 and hg >= 1:
            pe.wait_ge(a.o_copied, hg)
        for g in range(GRP):
            mm = pe.matmul(m.bank[32 * g:32 * g + 32, 5, lo:S], a.v(GRP * hg + g, kt),
                           a.probs[:, (GRP * n + g) % 8, 0:S - lo], start=(kt == 0),
                           stop=(kt == NT - 1), tile_position=(0, 32 * g))
        mm.then_inc(a.valued, 1)

    def turn_output(hg):
        pe.wait_ge(a.o_copied, hg + 1)
        if hg >= 1:
            pe.wait_ge(a.normed, hg)
        for qt in range(NT):
            mm = pe.transpose(m.bank[:, 7, qt * P:(qt + 1) * P], a.ost[:, hg % 2, qt * P:(qt + 1) * P],
                              m.ident[:, :])
        mm.then_inc(a.o_turned, 1)

    def ahead(u):
        if u < UNITS:
            scores(u)
        if u % 16 == TURN_AT and 16 < u < UNITS + 16:
            turn_maxima(u // 16 - 1)

    stacks_ready(pe)
    for u in range(AHEAD):
        ahead(u)
    for n in range(NT * NG):
        hg, kt = divmod(n, NT)
        for v in range(GRP * kt, GRP * kt + GRP):
            ahead(16 * hg + v + AHEAD)
            shifted_scores(hg, v)
        if n >= 1:
            values(n - 1)
        if n >= 5 and n % NT == 1:
            turn_output(n // NT - 1)
    values(NT * NG - 1)
    turn_output(NG - 1)


def attend_vector(dve, m, a):
    def maximum(u):
        hg, qt, g = max_unit(u)
        v = GRP * qt + g
        dve.wait_ge(a.scored, u + 1)
        dve.tensor_reduce(m.mx[:, hg % 2, v:v + 1], m.bank[:, u % 2, 0:width_s(a, qt)], AX.X,
                          ALU.max).then_inc(a.maxed, 1)

    def split_maxima(hg):
        mx = m.mx[:, hg % 2, :].rearrange("p (t g) -> p t g", g=GRP)
        rest = m.mr[:, hg % 2, :].rearrange("p (t g) -> p t g", g=GRP)
        part = [m.mp[:, hg % 2, :, GRP * r:GRP * r + GRP] for r in range(3)]
        dve.wait_ge(a.maxed, 16 * (hg + 1))
        dve.tensor_copy(part[0], mx).then_inc(a.m_parts, 1)
        dve.wait_ge(a.m_parts, 3 * hg + 1)
        dve.tensor_tensor(rest, mx, part[0], ALU.subtract).then_inc(a.m_rest, 1)
        dve.wait_ge(a.m_rest, hg + 1)
        dve.tensor_copy(part[1], rest).then_inc(a.m_parts, 1)
        dve.wait_ge(a.m_parts, 3 * hg + 2)
        dve.tensor_tensor(part[2], rest, part[1], ALU.subtract).then_inc(a.m_parts, 1)

    def copy_maxima(hg):
        dve.wait_ge(a.m_turned, hg + 1)
        if hg >= 2:
            dve.wait_ge(a.m_placed, 48 * (hg - 1))
        dve.tensor_copy(m.mT[:, hg % 2, :], m.bankb[0:3 * GRP, 6, 0:S]).then_inc(a.m_copied, 1)

    def normalize(hg):
        sums = m.bank[:, 7, :].rearrange("p (t g e) -> p t g e", t=NT, g=GRP)
        recip = m.recip[:, :].rearrange("p (t g) -> p t g", g=GRP)
        w = GRP * a.vdim
        out = a.o[:, :, hg * w:(hg + 1) * w].rearrange("p t (g e) -> p t g e", g=GRP)
        dve.wait_ge(a.o_turned, hg + 1)
        dve.reciprocal(recip, sums[:, :, :, a.vdim]).then_inc(a.recips, 1)
        dve.wait_ge(a.recips, hg + 1)
        dve.tensor_tensor(out, sums[:, :, :, 0:a.vdim],
                          recip.unsqueeze(3).to_broadcast([P, NT, GRP, a.vdim]),
                          ALU.mult).then_inc(a.normed, 1)

    def ahead(u):
        if u < UNITS:
            maximum(u)
        if u % 16 == 15 and u < UNITS:
            split_maxima(u // 16)
        if u % 16 == COPY_AT and 16 < u < UNITS + 16:
            copy_maxima(u // 16 - 1)

    for u in range(AHEAD):
        ahead(u)
    for u in range(UNITS):
        ahead(u + AHEAD)
        if u % 16 == 9 and u > 16:
            normalize(u // 16 - 1)
    normalize(NG - 1)


def attend_scalar(act, m, a):
    def copy_output(hg):
        act.wait_ge(a.valued, NT * (hg + 1))
        if hg >= 2:
            act.wait_ge(a.o_turned, hg - 1)
        act.activation(a.ost[:, hg % 2, :], m.bank[:, 5, :], ACT.Copy).then_inc(a.o_copied, 1)

    for n in range(NT * NG):
        w = S - first_t(a, n % NT)
        for g in range(GRP):
            u = GRP * n + g
            act.wait_ge(a.shifted, u + 1)
            if u >= 8:
                act.wait_ge(a.valued, n - 1)
            act.activation(a.probs[:, u % 8, 0:w], m.bank[:, 2 + u % 3, 0:w], ACT.Exp,
                           scale=a.scale).then_inc(a.exped, 1)
        if n >= 4 and n % NT == 0:
            copy_output(n // NT - 1)
    copy_output(NG - 1)


def attend_sync(sp, m, a, rows):
    for hg in range(NG):
        sp.wait_ge(a.m_copied, hg + 1)
        for r in range(3):
            sp.dma_start(rows(hg, r), m.mT[GRP * r:GRP * r + GRP, hg % 2, :]).then_inc(a.m_placed, 16)



def lots(kv_heads):
    return [(n, hb) for n in range(2 * NT) for hb in range((kv_heads if n % 2 else H) // 8)]


def lots_before(kv_heads, n):
    return sum(1 for x, _ in lots(kv_heads) if x < n)


def projection_bank(t, w):
    return (6 * (t % 2) + w) if w < 2 else 2 + t % 2


def project_tensor(pe, m, s, a, kv_heads, rhs, q_waits, tq, tk):
    order = lots(kv_heads)

    def turn(n):
        pe.wait_ge(a.stacked, n + 1)
        if n == 0:
            pe.wait_ge(a.consts, 4)
        for j, (x, hb) in enumerate(order):
            if x != n:
                continue
            if j >= 2:
                pe.wait_ge((a.placed_dve, a.placed_act)[j % 2], j // 2)
            t, rows = (tk, 99) if n % 2 else (tq, 96)
            for h in range(8):
                mm = pe.transpose(m.bankb[0:rows, 4 + j % 2, h * P:(h + 1) * P],
                                  t[:, 8 * hb + h, 0:rows], m.identb[:, :])
            mm.then_inc(a.turned, 1)

    def project(t, ws):
        pe.wait_ge(s.ln_copied, NT * a.i + t + 1)
        for w in ws:
            if t == 0:
                q_waits(pe, w)
            if t == 1 and w < 2:
                pe.wait_ge(s.ln_copied, NT * a.i + NT)
            if w < 2 and t >= 2:
                pe.wait_ge(a.rotated, 2 * (t - 2) + w + 1)
            if w == 2 and t >= 2:
                pe.wait_ge(a.v_read, t - 1)
            bank = projection_bank(t, w)
            for c in range(NC):
                r = rhs(w, c)
                out = m.bank[:, bank, 0:r.shape[1] * HD].rearrange("p (h d) -> p h d", d=HD)
                mm = pe.matmul(out, m.xT[:, c, t * P:(t + 1) * P], r, start=(c == 0), stop=(c == NC - 1))
            mm.then_inc(a.projected, 1)

    queries, others = ((0,), (1, 2)) if a.rope else ((0,), ())
    for t in range(2):
        project(t, queries + others)
    for t in range(NT):
        turn(2 * t)
        if t + 2 < NT:
            project(t + 2, queries)
        turn(2 * t + 1)
        if t + 2 < NT and others:
            project(t + 2, others)


def project_vector(dve, m, s, a, kv_heads, rq, rr, tq, tk, q, k):
    order = lots(kv_heads)

    def heads(n):
        return kv_heads if n % 2 else H

    def rotate_parts(n):
        t, w = divmod(n, 2)
        if not a.rope:
            return
        dve.wait_ge(a.projected, 3 * t + w + 1)
        bank = m.bank[:, projection_bank(t, w), :]
        x = bank.rearrange("p (h d) -> p h d", h=H)
        pair = bank.rearrange("p (h d z) -> p h d z", h=H, z=2)
        rbp = m.rb.rearrange("p (h d z) -> p h d z", h=H, z=2)
        sin = m.sin[:, t, :].rearrange("p (d z) -> p d z", z=2)
        if n >= 1:
            dve.wait_ge(a.rotated, n)
        else:
            dve.wait_ge(s.consts_loaded, s.n_consts)
        dve.tensor_tensor(m.ra.rearrange("p (h d) -> p h d", h=H), x,
                          m.cos[:, t, :].unsqueeze(1).to_broadcast([P, H, HD]), ALU.mult).then_inc(a.rope_a, 1)
        for z in range(2):
            dve.tensor_tensor(rbp[:, :, :, z], pair[:, :, :, 1 - z],
                              sin[:, :, z].unsqueeze(1).to_broadcast([P, H, HD // 2]),
                              ALU.mult).then_inc(a.rope_b, 1)

    def rotate(n):
        t, w = divmod(n, 2)
        width = heads(n) * HD
        if not a.rope:
            if w:
                dve.wait_ge(a.kv_loaded, 64 * NT)
            else:
                dve.wait_ge(a.projected, t + 1)
            if n >= 2:
                dve.wait_ge(a.split1, n - 1)
            dve.tensor_copy(rq[:, n % 2, 0:width], m.kt[:, t, :] if w else m.bank[:, projection_bank(t, 0), :])\
               .then_inc(a.rotated, 1)
            return
        dve.wait_ge(a.rope_a, n + 1)
        dve.wait_ge(a.rope_b, 2 * n + 2)
        if n >= 2:
            dve.wait_ge(a.split1, n - 1)
        dve.tensor_tensor(rq[:, n % 2, :], m.ra, m.rb, ALU.add).then_inc(a.rotated, 1)

    def stack(n, slots):
        return (tk if n % 2 else tq)[:, :, slots[0] * HD:(slots[0] + 1) * HD]

    def rest(n):
        w = heads(n) * HD
        dve.wait_ge(a.split1, n + 1)
        if n >= 1:
            dve.wait_ge(a.stacked, n)
        dve.tensor_tensor(rr[:, 0:w].rearrange("p (h d) -> p h d", d=HD),
                          rq[:, n % 2, 0:w].rearrange("p (h d) -> p h d", d=HD),
                          stack(n, (0,)), ALU.subtract).then_inc(a.rest, 1)

    def last_part(n):
        w = heads(n) * HD
        dve.wait_ge(a.split2, n + 1)
        dve.tensor_tensor(stack(n, (2,) if n % 2 else (5,)),
                          rr[:, 0:w].rearrange("p (h d) -> p h d", d=HD),
                          stack(n, (1,) if n % 2 else (3,)), ALU.subtract).then_inc(a.stacked, 1)

    def place(n):
        for j, (x, hb) in enumerate(order):
            if x == n and j % 2 == 0:
                rows, out = (99, k) if n % 2 else (96, q)
                dve.wait_ge(a.turned, j + 1)
                dve.tensor_copy(out[0:rows, 8 * hb:8 * hb + 8, (n // 2) * P:(n // 2 + 1) * P],
                                m.bankb[0:rows, 4 + j % 2, :].rearrange("p (h n) -> p h n", h=8))\
                   .then_inc(a.placed_dve, 1)

    rotate_parts(0)
    rotate(0)
    for n in range(2 * NT):
        if n >= 2:
            place(n - 2)
        if n + 1 < 2 * NT:
            rotate_parts(n + 1)
        rest(n)
        if n + 1 < 2 * NT:
            rotate(n + 1)
        last_part(n)
    place(2 * NT - 2)
    place(2 * NT - 1)


def project_scalar(act, m, s, a, kv_heads, rq, rr, tq, tk, v, q, k):
    order = lots(kv_heads)

    def split(n, first):
        nh = kv_heads if n % 2 else H
        stk = (tk if n % 2 else tq)[:, :, 0:6 * HD].rearrange("p h (j d) -> p h j d", d=HD)
        src = (rq[:, n % 2, 0:nh * HD] if first else rr[:, 0:nh * HD]).rearrange("p (h d) -> p h d", d=HD)
        if n % 2:
            runs = [(0, 1), (3, 4), (5, 6)] if first else [(1, 2), (4, 5)]
        else:
            runs = [(0, 3)] if first else [(3, 5)]
        if first:
            act.wait_ge(a.rotated, n + 1)
            if n >= 2:
                act.wait_ge(a.turned, lots_before(kv_heads, n - 1))
        else:
            act.wait_ge(a.rest, n + 1)
        for j, (lo, hi) in enumerate(runs):
            one = act.activation(stk[:, :, lo:hi, :], src.unsqueeze(2).to_broadcast([P, nh, hi - lo, HD]),
                                 ACT.Copy)
        one.then_inc(a.split1 if first else a.split2, 1)

    def place(n):
        for j, (x, hb) in enumerate(order):
            if x == n and j % 2 == 1:
                rows, out = (99, k) if n % 2 else (96, q)
                act.wait_ge(a.turned, j + 1)
                act.activation(out[0:rows, 8 * hb:8 * hb + 8, (n // 2) * P:(n // 2 + 1) * P],
                               m.bankb[0:rows, 4 + j % 2, :].rearrange("p (h n) -> p h n", h=8),
                               ACT.Copy).then_inc(a.placed_act, 1)

    for n in range(2 * NT):
        if n >= 2:
            place(n - 2)
        split(n, True)
        if n % 2 == 0 and a.rope:
            t = n // 2
            act.wait_ge(a.projected, 3 * t + 3)
            act.activation(v[:, t, :, 0:HD],
                           m.bank[:, 2 + t % 2, 0:kv_heads * HD].rearrange("p (h d) -> p h d", d=HD),
                           ACT.Copy).then_inc(a.v_read, 1)
        split(n, False)
    place(2 * NT - 2)
    place(2 * NT - 1)


def project_gpsimd(pool, m, s, a, v, tk, kv_heads):
    pool.wait_ge(s.bias_made, 1)
    pool.wait_ge(s.wcomb_made, 1)
    pool.wait_ge(s.ln_rstd, NT)
    pool.memset(m.arena[96:P, 8192:16384 + kv_heads * S // 2], 0.0).then_inc(a.consts, 1)
    pool.wait_ge(a.consts, 1)
    pool.memset(v[:, :, :, HD:32], 0.0).then_inc(a.consts, 1)
    pool.wait_ge(a.consts, 2)
    pool.memset(v[:, :, :, HD:HD + 1], 1.0).then_inc(a.consts, 1)
    pool.memset(tk[:, :, 96:99], -1.0).then_inc(a.consts, 1)


def output_tensor(pe, m, s, a, w, wait_w):
    pe.wait_ge(a.normed, NG)
    for t in range(NT):
        if t >= 2:
            pe.wait_ge(a.out_copied, t - 1)
        for c in range(NC):
            mm = pe.transpose(m.bank[:, 6 + t % 2, c * P:(c + 1) * P], a.o[:, t, c * P:(c + 1) * P],
                              m.ident[:, :])
        mm.then_inc(a.out_turned, 1)
    wait_w(pe)
    for t in range(NT):
        pe.wait_ge(a.out_copied, t + 1)
        if t >= 2:
            pe.wait_ge(s.x_updated, NT * a.i + t - 1)
        for c in range(NC):
            mm = pe.matmul(m.bank[:, t % 2, :], m.xT[:, c, t * P:(t + 1) * P], w[:, c, :],
                           start=(c == 0), stop=(c == NC - 1))
        mm.then_inc(a.out_made, 1)


def output_scalar(act, m, a):
    for t in range(NT):
        act.wait_ge(a.out_turned, t + 1)
        act.activation(m.xT[:, :, t * P:(t + 1) * P],
                       m.bank[:, 6 + t % 2, :].rearrange("p (c n) -> p c n", c=NC),
                       ACT.Copy).then_inc(a.out_copied, 1)



def latent_tensor(pe, m, s, a):
    for t in range(NT):
        pe.wait_ge(s.ln_copied, NT * a.i + t + 1)
        for c in range(NC):
            mm = pe.matmul(m.bank[:, 0, 16 * t:16 * t + 16], m.xT[:, c, t * P:(t + 1) * P],
                           m.wlat[:, c, :], start=(c == 0), stop=(c == NC - 1))
    mm.then_inc(s.lat_made, 1)
    pe.wait_ge(s.lat_ready, 1)
    for t in range(NT):
        mm = pe.transpose(m.bank[0:QLAT, 1, t * P:(t + 1) * P], m.lat[:, t, 0:QLAT], m.ident[:, :])
    mm.then_inc(s.cq_turned, 1)
    pe.wait_ge(s.cq_copied, 1)
    for t in range(NT):
        mm = pe.matmul(m.bank[:, 2, t * P:(t + 1) * P], m.cqT[0:QLAT, t * P:(t + 1) * P], m.wqk[:, :],
                       start=True, stop=True)
    mm.then_inc(a.projected, 1)
    pe.wait_ge(s.klat_stacked, 10)
    pe.wait_ge(a.consts, 5)
    for t in range(NT):
        mm = pe.transpose(m.bankb[:, 1, t * P:(t + 1) * P],
                          m.tkM[:, t, :, :].rearrange("p r e -> p (r e)"), m.identb[:, :])
    mm.then_inc(s.klat_turned, 1)
    for t in range(NT):
        pe.wait_ge(a.stacked, t + 1)
        if t >= 2:
            pe.wait_ge(a.placed_dve, t - 1)
        for hg in range(NG):
            mm = pe.transpose(m.bankb[:, 4 + t % 2, hg * P:(hg + 1) * P],
                              m.tqM[:, GRP * hg:GRP * hg + GRP, :].rearrange("p h e -> p (h e)"),
                              m.identb[:, :])
        mm.then_inc(a.turned, 1)


def latent_vector(dve, m, s, a):
    dve.wait_ge(s.lat_made, 1)
    dve.tensor_tensor(m.lat, m.bank[:, 0, 0:64].rearrange("p (t e) -> p t e", t=NT),
                      m.blat[:, :].unsqueeze(1).to_broadcast([P, NT, 16]), ALU.add).then_inc(s.lat_ready, 1)
    dve.wait_ge(s.lat_ready, 1)
    ckv = m.lat[:, :, QLAT:QLAT + LAT]
    dve.tensor_copy(m.kp[:, 0], ckv).then_inc(s.klat_stacked, 1)
    dve.wait_ge(s.klat_stacked, 1)
    dve.tensor_tensor(m.kr, ckv, m.kp[:, 0], ALU.subtract).then_inc(s.klat_stacked, 1)
    dve.wait_ge(s.klat_stacked, 2)
    dve.tensor_copy(m.kp[:, 1], m.kr).then_inc(s.klat_stacked, 1)
    dve.wait_ge(s.klat_stacked, 3)
    dve.tensor_tensor(m.kp[:, 2], m.kr, m.kp[:, 1], ALU.subtract).then_inc(s.klat_stacked, 1)
    dve.wait_ge(s.klat_stacked, 4)
    for j, part in enumerate((0, 1, 2, 0, 1, 0)):
        dve.tensor_copy(m.tkM[:, :, :, LAT * j:LAT * j + LAT],
                        m.kp[:, part].unsqueeze(2).to_broadcast([P, NT, 4, LAT])).then_inc(s.klat_stacked, 1)
    dve.wait_ge(a.consts, 5)
    dve.tensor_copy(m.vM[:, :, 0:LAT], ckv).then_inc(s.vlat_made, 1)
    rr = m.rrM.rearrange("p (h d) -> p h d", d=LAT)
    for t in range(NT):
        if t == 0:
            dve.wait_ge(a.projected, 1)
        dve.tensor_tensor(m.rqM[:, t % 2, :], m.bank[:, 2, t * P:(t + 1) * P], m.bqk[:, :],
                          ALU.add).then_inc(a.rotated, 1)
        dve.wait_ge(a.split1, t + 1)
        dve.tensor_tensor(rr, m.rqM[:, t % 2, :].rearrange("p (h d) -> p h d", d=LAT),
                          m.tqM[:, :, 0:LAT], ALU.subtract).then_inc(a.rest, 1)
        dve.wait_ge(a.split2, t + 1)
        dve.tensor_tensor(m.tqM[:, :, 5 * LAT:6 * LAT], rr, m.tqM[:, :, 3 * LAT:4 * LAT],
                          ALU.subtract).then_inc(a.stacked, 1)
        if t == 0:
            dve.wait_ge(s.klat_turned, 1)
            for g in range(GRP):
                dve.tensor_copy(m.kM[32 * g:32 * g + 32, g, :], m.bankb[32 * g:32 * g + 32, 1, 0:S])\
                   .then_inc(s.klat_placed, 1)
        dve.wait_ge(a.turned, t + 1)
        dve.tensor_copy(m.qM[:, :, t * P:(t + 1) * P],
                        m.bankb[:, 4 + t % 2, :].rearrange("p (h n) -> p h n", h=NG)).then_inc(a.placed_dve, 1)


def latent_scalar(act, m, s, a):
    act.wait_ge(s.cq_turned, 1)
    act.activation(m.cqT[0:QLAT, :], m.bank[0:QLAT, 1, :], ACT.Copy).then_inc(s.cq_copied, 1)
    slots = m.tqM[:, :, 0:24].rearrange("p h (j d) -> p h j d", d=LAT)
    for t in range(NT):
        act.wait_ge(a.rotated, t + 1)
        if t >= 1:
            act.wait_ge(a.turned, t)
        src = m.rqM[:, t % 2, :].rearrange("p (h d) -> p h d", d=LAT)
        act.activation(slots[:, :, 0:3, :], src.unsqueeze(2).to_broadcast([P, H, 3, LAT]),
                       ACT.Copy).then_inc(a.split1, 1)
        act.wait_ge(a.rest, t + 1)
        src = m.rrM.rearrange("p (h d) -> p h d", d=LAT)
        act.activation(slots[:, :, 3:5, :], src.unsqueeze(2).to_broadcast([P, H, 2, LAT]),
                       ACT.Copy).then_inc(a.split2, 1)


def latent_gpsimd(pool, m, s, a):
    pool.wait_ge(s.ln_copied, NT * a.i + 1)
    pool.memset(m.vM[:, :, LAT:32], 0.0).then_inc(a.consts, 1)
    pool.wait_ge(a.consts, 1)
    pool.memset(m.vM[:, :, LAT:LAT + 1], 1.0).then_inc(a.consts, 1)
    pool.memset(m.tkM[:, :, :, 24:32], -1.0).then_inc(a.consts, 1)
    pool.memset(m.tqM[:, :, 24:32], 0.0).then_inc(a.consts, 1)
    pool.memset(m.kM, 0.0).then_inc(a.consts, 1)


def latent_output_tensor(pe, m, s, a):
    pe.wait_ge(a.normed, NG)
    for t in range(NT):
        mm = pe.transpose(m.bank[:, 6, t * P:(t + 1) * P], a.o[:, t, :], m.ident[:, :])
    mm.then_inc(a.out_turned, 1)
    pe.wait_ge(a.out_copied, 1)
    for t in range(NT):
        if t >= 2:
            pe.wait_ge(s.x_updated, NT * a.i + t - 1)
        pe.matmul(m.bank[:, t % 2, :], m.oMT[:, t * P:(t + 1) * P], m.wcomb[:, :],
                  start=True, stop=True).then_inc(a.out_made, 1)


def latent_output_scalar(act, m, a):
    act.wait_ge(a.out_turned, 1)
    act.activation(m.oMT, m.bank[:, 6, :], ACT.Copy).then_inc(a.out_copied, 1)


class Feed:

    def __init__(self, sem, i):
        self.i = i
        self.p_made = sem("ff_p_made")
        self.p_copied = sem("ff_p_copied")
        self.h_made = sem("ff_h_made")
        self.gated = sem("ff_gated")
        self.acted = sem("ff_acted")
        self.z_made = sem("ff_z_made")
        self.z_copied = sem("ff_z_copied")
        self.out_made = sem("ff_out_made")


def inner(j):
    return min(P, INTER - P * j)


def feed_tensor(pe, m, s, f):
    pe.wait_ge(s.ln_copied, NT * f.i + NT)
    if f.i == LN_F1:
        pe.wait_ge(s.consts_loaded, s.n_consts)
    for c in range(NC):
        mm = pe.matmul(m.bank[:, 0, :], m.U1[:, c, :], m.xT[:, c, :], start=(c == 0), stop=(c == NC - 1))
    mm.then_inc(f.p_made, 1)
    pe.wait_ge(f.p_copied, 1)

    def second(j):
        pe.wait_ge(f.acted, j + 1)
        mm = pe.matmul(m.bank[:, 5, :], m.U2[0:inner(j), j, :], m.act[0:inner(j), j % 3, :],
                       start=(j == 0), stop=(j == NF - 1))
        if j == NF - 1:
            mm.then_inc(f.z_made, 1)

    for j in range(NF):
        w = inner(j)
        for z in range(2):
            if j >= 2:
                pe.wait_ge((f.gated, f.acted)[z], j - 1)
            pe.matmul(m.bank[0:w, 1 + 2 * z + j % 2, :], m.V1[:, z * INTER + j * P:z * INTER + j * P + w],
                      m.pT, start=True, stop=True).then_inc(f.h_made, 1)
        if j >= 1:
            second(j - 1)
    second(NF - 1)
    pe.wait_ge(f.z_copied, 1)
    for t in range(NT):
        if t >= 2:
            pe.wait_ge(s.x_updated, NT * f.i + t - 1)
        pe.matmul(m.bank[:, 6 + t % 2, :], m.zT[:, t * P:(t + 1) * P], m.V2[:, :],
                  start=True, stop=True).then_inc(f.out_made, 1)


def feed_scalar(act, m, s, f):
    act.wait_ge(f.p_made, 1)
    act.activation(m.pT, m.bank[:, 0, :], ACT.Copy).then_inc(f.p_copied, 1)
    for j in range(NF):
        w = inner(j)
        act.wait_ge(f.h_made, 2 * j + 1)
        if j >= 2:
            act.wait_ge(f.acted, j - 1)
        act.activation(m.sg[0:w, j % 2, :], m.bank[0:w, 1 + j % 2, :], ACT.Silu,
                       bias=m.b1[0:w, 0, j:j + 1]).then_inc(f.gated, 1)
    act.wait_ge(f.z_made, 1)
    act.activation(m.zT, m.bank[:, 5, :], ACT.Copy).then_inc(f.z_copied, 1)


def feed_vector(dve, m, s, f):
    for j in range(NF):
        w = inner(j)
        dve.wait_ge(f.h_made, 2 * j + 2)
        dve.wait_ge(f.gated, j + 1)
        dve.scalar_tensor_tensor(m.act[0:w, j % 3, :], m.bank[0:w, 3 + j % 2, :], m.b1[0:w, 1, j:j + 1],
                                 m.sg[0:w, j % 2, :], ALU.add, ALU.mult).then_inc(f.acted, 1)



def nf4_tensor(pe, m, s, i, made):
    if i == LN_N1:
        pe.wait_ge(s.nf4_ready, NC)
    for t in range(NT):
        pe.wait_ge(s.ln_copied, NT * i + t + 1)
        for c in range(NC):
            mm = pe.matmul(m.bank[:, t, :], m.xT[:, c, t * P:(t + 1) * P], m.nf4w[:, c, :],
                           start=(c == 0), stop=(c == NC - 1))
        mm.then_inc(made, 1)



def kv_tensor(pe, m, s, wkv):
    pe.wait_ge(s.wkv_loaded, 16)
    for t in range(NT):
        pe.wait_ge(s.ln_copied, NT * LN_KV + t + 1)
        for c in range(NC):
            mm = pe.matmul(m.bank[:, t, 0:256], m.xT[:, c, t * P:(t + 1) * P], wkv[:, c, :],
                           start=(c == 0), stop=(c == NC - 1))
        mm.then_inc(s.kv_made, 1)


def kv_scalar(act, m, s):
    for t in range(NT):
        act.wait_ge(s.kv_made, t + 1)
        act.activation(m.kvo[:, t, :], m.bank[:, t, 0:256], ACT.Copy).then_inc(s.kv_copied, 1)



def scan_tensor(pe, m, s):
    def project(j):
        if j >= 3:
            if j - 3 < NM:
                pe.wait_ge(s.convolved, 4 * (j - 3 + 1))
            else:
                pe.wait_ge(s.gates, j - 3 - NM + 1)
        for c in range(NC):
            mm = pe.matmul(m.bank[:, j % 3, :], m.win[:, j // NM, c, (j % NM) * P:(j % NM + 1) * P],
                           m.xT[:, c, :], start=(c == 0), stop=(c == NC - 1))
        mm.then_inc(s.inner_made, 1)

    pe.wait_ge(s.win_loaded, 32)
    pe.wait_ge(s.ln_copied, NT * LN_S + NT)
    for j in range(NM + 2):
        project(j)
    pe.wait_ge(s.wx_loaded, 32)
    pe.wait_ge(s.xs_made, NM)
    for t in range(NT):
        for j in range(NM):
            mm = pe.matmul(m.bank[:, 3, 64 * t:64 * t + 64], m.xs[:, j, t * P:(t + 1) * P], m.wx[:, j, :],
                           start=(j == 0), stop=(j == NM - 1))
    mm.then_inc(s.ssm_made, 1)
    project(NM + 2)
    project(NM + 3)
    pe.wait_ge(s.ssm_normed, 3)
    for t in range(NT):
        mm = pe.transpose(m.bank[0:64, 4, t * P:(t + 1) * P], m.ssm[:, t, :], m.ident[:, :])
    mm.then_inc(s.ssm_turned, 1)
    project(NM + 4)
    pe.wait_ge(s.ssm_copied, 1)
    for j in range(NM):
        if j >= 2:
            pe.wait_ge(s.z_read, 2 * (j - 2) + 1)
        pe.matmul(m.bank[:, 5 + j % 2, :], m.wdt[0:RDT, j * P:(j + 1) * P], m.ssmT[0:RDT, :],
                  start=True, stop=True).then_inc(s.z_made, 1)
    for j in range(5, NM):
        project(NM + j)
    for q in range(2 * NM):
        half, j = divmod(q, NM)
        if q >= 2:
            pe.wait_ge(*((s.y_kept, q - 1) if q - 2 < NM else (s.y_made, q - 1 - NM)))
        pe.wait_ge((s.skipped, s.y_kept)[half], j + 1)
        pe.matmul(m.bank[:, q % 2, :], m.ident[:, :], m.y(j), start=True, stop=False)
        for k in range(4):
            u = 4 * q + k
            pe.wait_ge(s.weighted, u + 1)
            for x in range(2):
                mm = pe.matmul(m.bank[:, q % 2, :], m.ident[:, :], m.state[:, u % 2, x, :],
                               start=False, stop=(k == 3 and x == 1))
            mm.then_inc(s.summed, 1)
    pe.wait_ge(s.wout_loaded, 16)
    pe.wait_ge(s.y_made, NM)
    for t in range(NT):
        for j in range(NM):
            mm = pe.matmul(m.bank[:, 2 + t, :], m.y(j)[:, t * P:(t + 1) * P], m.wout[:, j, :],
                           start=(j == 0), stop=(j == NM - 1))
        mm.then_inc(s.scan_out_made, 1)


def scan_scalar(act, m, s):
    for j in range(NM):
        act.wait_ge(s.convolved, 4 * (j + 1))
        act.activation(m.xs[:, j, :], m.conv[:, j % 2, :], ACT.Silu).then_inc(s.xs_made, 1)
    def gate(j):
        act.wait_ge(s.inner_made, NM + j + 1)
        act.activation(m.gate[:, j, :], m.bank[:, (NM + j) % 3, :], ACT.Silu).then_inc(s.gates, 1)

    for j in range(4):
        gate(j)
    act.wait_ge(s.ssm_turned, 1)
    act.activation(m.ssmT[0:64, :], m.bank[0:64, 4, :], ACT.Copy).then_inc(s.ssm_copied, 1)
    gate(4)
    for j in range(NM):
        act.wait_ge(s.z_read, 2 * (j + 1))
        act.activation(m.dt[:, j, :], m.dt[:, j, :], ACT.Exp).then_inc(s.dt_steps, 1)
    for j in range(NM):
        act.wait_ge(s.one_plus, j + 1)
        act.activation(m.plus(j), m.plus(j), ACT.Ln).then_inc(s.log_made, 1)
    for j in range(5, NM):
        gate(j)
    for j in range(NM):
        act.activation(m.y(j), m.xs[:, j, :], ACT.Identity, scale=m.Dskip[:, j:j + 1]).then_inc(s.skipped, 1)

    def keep(j):
        act.wait_ge(s.summed, 4 * (j + 1))
        act.activation(m.y(j), m.bank[:, j % 2, :], ACT.Copy).then_inc(s.y_kept, 1)

    for q in range(2 * NM):
        half, j = divmod(q, NM)
        for k in range(4):
            u = 4 * q + k
            if u == 0:
                act.wait_ge(s.decay_cleared, 2)
            if q < NM and k == 0:
                act.wait_ge(s.dt_made, j + 1)
            if u >= 2:
                act.wait_ge(s.scanned, u - 1)
            for x in range(2):
                n = 8 * half + 2 * k + x
                one = act.activation(m.decay[:, u % 2, x, 1:S], m.dt[:, j, 1:S], ACT.Exp,
                                     scale=m.A[:, j, n:n + 1])
            one.then_inc(s.decays, 1)
            if k == 2 and 1 <= q <= NM:
                keep(q - 1)


def scan_gpsimd(pool, m, s):
    for r, (w, e) in enumerate(((RDT, 0), (NS, 1), (NS, 2))):
        pool.wait_ge(s.ssm_squares, r + 1)
        pool.tensor_scalar(m.rms[:, :, e], m.rms[:, :, e], 1.0 / w, EPS_RMS, ALU.mult,
                           ALU.add).then_inc(s.rms_steps, 1)
        pool.wait_ge(s.rms_steps, 2 * r + 1)
        pool.tensor_tensor(m.rms[:, :, e], m.rms[:, :, e], m.minus_half[:, 0:NT], ALU.pow)\
            .then_inc(s.rms_steps, 1)
    pool.wait_ge(s.dt_made, NM)
    pool.wait_ge(s.log_made, NM)
    for r in range(2):
        pool.memset(m.decay[:, r, :, 0:1], 0.0).then_inc(s.decay_cleared, 1)
    for q in range(2 * NM):
        half, j = divmod(q, NM)
        if half == 0:
            pool.wait_ge(s.du_made, j + 1)
        for k in range(4):
            u = 4 * q + k
            pool.wait_ge(s.rep_b[k], 16 * (half + 1))
            if u >= 2:
                pool.wait_ge(s.scanned, u - 1)
            pool.tensor_tensor(m.drive[:, u % 2], m.xs[:, j, :].unsqueeze(1).to_broadcast([P, 2, S]),
                               m.brep[:, 2 * k:2 * k + 2, :], ALU.mult).then_inc(s.driven, 1)


def scan_vector(dve, m, s):
    for j in range(NM):
        w = m.convw[:, j, :]
        x = m.bank[:, j % 3, :]
        c = m.conv[:, j % 2, :]
        dve.wait_ge(s.inner_made, j + 1)
        if j >= 2:
            dve.wait_ge(s.xs_made, j - 1)
        dve.tensor_scalar(c, x, w[:, 3:4], m.convb[:, j:j + 1], ALU.mult, ALU.add).then_inc(s.convolved, 1)
        for k in range(1, 4):
            dve.wait_ge(s.convolved, 4 * j + k)
            dve.scalar_tensor_tensor(c[:, k:S], x[:, 0:S - k], w[:, 3 - k:4 - k], c[:, k:S], ALU.mult,
                                     ALU.add).then_inc(s.convolved, 1)
    dve.wait_ge(s.ssm_made, 1)
    dve.tensor_copy(m.ssm, m.bank[:, 3, 0:256].rearrange("p (t e) -> p t e", t=NT)).then_inc(s.ssm_steps, 1)
    dve.wait_ge(s.ssm_steps, 1)
    dve.tensor_tensor(m.ssq, m.ssm, m.ssm, ALU.mult).then_inc(s.ssm_steps, 1)
    dve.wait_ge(s.ssm_steps, 2)
    parts = ((0, RDT), (RDT, RDT + NS), (RDT + NS, RDT + 2 * NS))
    for r, (lo, hi) in enumerate(parts):
        dve.tensor_reduce(m.rms[:, :, r:r + 1], m.ssq[:, :, lo:hi], AX.X, ALU.add).then_inc(s.ssm_squares, 1)
    for r, (lo, hi) in enumerate(parts):
        dve.wait_ge(s.rms_steps, 2 * r + 2)
        dve.tensor_tensor(m.ssm[:, :, lo:hi], m.ssm[:, :, lo:hi],
                          m.rms[:, :, r:r + 1].to_broadcast([P, NT, hi - lo]), ALU.mult).then_inc(s.ssm_normed, 1)
    for j in range(NM):
        dve.wait_ge(s.z_made, j + 1)
        dve.tensor_scalar(m.zdt[:, j, :], m.bank[:, 5 + j % 2, :], m.bdt[:, j:j + 1], None,
                          ALU.add).then_inc(s.z_read, 1)
        dve.wait_ge(s.z_read, 2 * j + 1)
        dve.scalar_tensor_tensor(m.dt[:, j, :], m.zdt[:, j, :], -1.0, m.zdt[:, j, :], ALU.mult,
                                 ALU.min).then_inc(s.z_read, 1)
    for j in range(NM):
        dve.wait_ge(s.dt_steps, j + 1)
        dve.tensor_scalar(m.plus(j), m.dt[:, j, :], 1.0, None, ALU.add).then_inc(s.one_added, 1)
        dve.wait_ge(s.one_added, j + 1)
        dve.scalar_tensor_tensor(m.dt[:, j, :], m.plus(j), -1.0, m.dt[:, j, :], ALU.add,
                                 ALU.subtract).then_inc(s.one_plus, 1)
    for j in range(NM):
        dve.wait_ge(s.log_made, j + 1)
        dve.tensor_tensor(m.dt[:, j, :], m.plus(j), m.dt[:, j, :], ALU.subtract).then_inc(s.logs, 1)
        dve.wait_ge(s.logs, j + 1)
        dve.scalar_tensor_tensor(m.dt[:, j, :], m.zdt[:, j, :], 0.0, m.dt[:, j, :], ALU.max,
                                 ALU.add).then_inc(s.dt_made, 1)

    def times_input(j):
        if j == 0:
            dve.wait_ge(s.dt_made, NM)
            dve.wait_ge(s.nf4_ready, NC)
        dve.wait_ge(s.skipped, j + 1)
        dve.tensor_tensor(m.xs[:, j, :], m.dt[:, j, :], m.xs[:, j, :], ALU.mult).then_inc(s.du_made, 1)

    def read_out(j):
        dve.wait_ge(s.summed, 4 * (NM + j + 1))
        dve.tensor_tensor(m.y(j), m.bank[:, (NM + j) % 2, :], m.gate[:, j, :], ALU.mult).then_inc(s.y_made, 1)

    times_input(0)
    for q in range(2 * NM):
        half = q // NM
        if q + 1 < NM:
            times_input(q + 1)
        for k in range(4):
            u = 4 * q + k
            dve.wait_ge(s.decays, u + 1)
            dve.wait_ge(s.driven, u + 1)
            if u >= 2:
                dve.wait_ge(s.summed, u - 1)
            flat = m.state[:, u % 2].rearrange("p j n -> p (j n)")
            dve.tensor_tensor_scan(flat, m.decay[:, u % 2].rearrange("p j n -> p (j n)"),
                                   m.drive[:, u % 2].rearrange("p j n -> p (j n)"), 0.0, ALU.mult,
                                   ALU.add).then_inc(s.scanned, 1)
            dve.wait_ge(s.scanned, u + 1)
            dve.wait_ge(s.rep_c[k], 16 * (half + 1))
            dve.tensor_tensor(m.state[:, u % 2], m.state[:, u % 2], m.crep[:, 2 * k:2 * k + 2, :],
                              ALU.mult).then_inc(s.weighted, 1)
        if q > NM:
            read_out(q - 1 - NM)
    read_out(NM - 1)


def scan_sync(sp, m, s, rows):
    sp.wait_ge(s.ssm_copied, 1)
    sp.dma_start(rows, m.ssmT[RDT:RDT + 2 * NS, :]).then_inc(s.rows_stored, 16)
    sp.wait_ge(s.rows_stored, 16)
    for half in range(2):
        for k in range(4):
            n = 8 * half + 2 * k
            if half:
                sp.wait_ge(s.driven, 4 * (NM - 1) + k + 1)
            else:
                sp.wait_ge(s.logs, 2 * k + 2)
            sp.dma_start(m.brep[:, 2 * k:2 * k + 2, :],
                         rows[n:n + 2, :].rearrange("(o n) s -> o n s", o=1).to_broadcast([P, 2, S]))\
              .then_inc(s.rep_b[k], 16)
            sp.wait_ge(*((s.weighted, 4 * (NM - 1) + k + 1) if half else (s.inner_made, 2 * NM)))
            sp.dma_start(m.crep[:, 2 * k:2 * k + 2, :],
                         rows[NS + n:NS + n + 2, :].rearrange("(o n) s -> o n s", o=1).to_broadcast([P, 2, S]))\
              .then_inc(s.rep_c[k], 16)



def dequantize(eng, m, s, c, absmax, loaded, steps, tmp, code):
    w = m.nf4w[:, c, :]
    eng.wait_ge(loaded, 48)
    n = 0
    for v, value in enumerate(NF4):
        if value == 0.0:
            continue
        eng.tensor_scalar(w if v == 0 else tmp, code, float(v), value, ALU.is_equal, ALU.mult).then_inc(steps, 1)
        n += 1
        eng.wait_ge(steps, n)
        if v:
            eng.tensor_tensor(w, w, tmp, ALU.add).then_inc(steps, 1)
            n += 1
            eng.wait_ge(steps, n)
    eng.tensor_tensor(w, w, absmax, ALU.mult).then_inc(s.nf4_ready, 1)


def setup_sync(sp, m, s, t):
    def load(out, src, signal=None):
        sp.dma_start(out, src).then_inc(signal or s.consts_loaded, 16)
        if signal is None:
            count[0] += 1

    def row(x):
        return x.rearrange("(o n) -> o n", o=1).to_broadcast([P, x.shape[0]])

    count = [0]
    for c in range(NC):
        load(m.nf_codes[c], t["codesT"][c * P:(c + 1) * P, :], s.codes_loaded[c])
        for z in range(2):
            load(m.nf_absmax[c][64 * z:64 * z + 64, :],
                 t["absmaxT"][2 * c + z:2 * c + z + 1, :].to_broadcast([64, D]), s.codes_loaded[c])
    load(m.cos[:, :, :], t["cos"].rearrange("(t p) e -> p t e", p=P))
    load(m.sin[:, :, :], t["sin"].rearrange("(t p) e -> p t e", p=P))
    sp.wait_ge(s.bd_cleared, 1)
    for h in range(8):
        load(m.bd[HD * h:HD * h + HD, :, LAT * h:LAT * h + LAT],
             t["Wv_uT"].rearrange("(c h d) j -> h d c j", c=NC, h=8)[h], s.latent_loaded)
    load(m.wo_lat, t["Wo_lat"].rearrange("(c p) n -> p c n", p=P), s.latent_loaded)
    load(m.bv, t["bv"], s.latent_loaded)
    load(m.bo_row, row(t["bo_lat"]), s.latent_loaded)
    load(m.U1[:, :, :], t["U1"].rearrange("(c p) r -> p c r", p=P))
    load(m.V1[:, :], t["V1"])
    last = P * (NF - 1)
    load(m.U2[:, 0:NF - 1, :], t["U2"][0:last, :].rearrange("(j p) r -> p j r", p=P))
    load(m.U2[0:INTER - last, NF - 1, :], t["U2"][last:INTER, :])
    load(m.V2[:, :], t["V2"])
    load(m.b1[:, :, :], t["b1"])
    load(m.bias[:, 0, :], row(t["b2"]))
    load(m.bias[:, 2, :], row(t["bias_nf4"]))
    load(m.bias[:, 3, :], row(t["bo_gqa"]))
    load(m.wlat[:, :, 0:QLAT], t["Wq_d"].rearrange("(c p) n -> p c n", p=P))
    load(m.wlat[:, :, QLAT:QLAT + LAT], t["Wkv_d"].rearrange("(c p) n -> p c n", p=P))
    load(m.blat[:, 0:QLAT], row(t["bq_d"]))
    load(m.blat[:, QLAT:QLAT + LAT], row(t["bkv_d"]))
    load(m.wqk[:, :], t["W_qk"])
    load(m.bqk[:, :], row(t["b_qk"]))
    load(m.convw[:, :, :], t["conv_w"].rearrange("(m p) k -> p m k", p=P))
    load(m.convb[:, :], t["conv_b"])
    load(m.bdt[:, :], t["b_dt"])
    load(m.Dskip[:, :], t["D"])
    load(m.alog, t["A_log"].rearrange("(m p) n -> p m n", p=P))
    assert 16 * count[0] == s.n_consts, count


def setup_gpsimd(pool, m, s):
    pool.memset(m.minus_half[:, :], -0.5).then_inc(s.ident_made, 1)
    pool.memset(m.bd, 0.0).then_inc(s.bd_cleared, 1)
    for x, value in ((m.ident, 1.0), (m.identb, 1.0), (m.maskS, 0.0), (m.maskT, 0.0)):
        pool.memset(x[:, :], value).then_inc(s.masks_cleared, 1)
    pool.wait_ge(s.masks_cleared, 4)
    for x, op, fill, sign in ((m.ident, ALU.is_equal, 0.0, 1), (m.identb, ALU.is_equal, 0.0, 1),
                              (m.maskS, ALU.is_ge, MASKED, 1), (m.maskT, ALU.is_ge, MASKED, -1)):
        pool.affine_select(out=x[:, :], in_=x[:, :], compare_op=op, fill=fill, base=0,
                           pattern=[[-sign, P]], channel_multiplier=sign).then_inc(s.ident_made, 1)
    dequantize(pool, m, s, 3, m.nf_absmax[3], s.codes_loaded[3], s.nf_steps[3], m.nf_tmps[1], m.nf_codes[3])


def setup_vector(dve, m, s):
    dve.wait_ge(s.latent_loaded, 11 * 16)
    for c in range(NC):
        dve.tensor_copy(m.bvb[:, c, :], m.bv[:, c:c + 1].to_broadcast([P, P])).then_inc(s.bvb_made, 1)
    for c in range(3):
        dequantize(dve, m, s, c, m.nf_absmax[c], s.codes_loaded[c], s.nf_steps[c], m.nf_tmps[0], m.nf_codes[c])
    dve.wait_ge(s.latent_bias, 1)
    dve.tensor_tensor(m.bias[:, 1, :], m.bank[:, 1, :], m.bo_row, ALU.add).then_inc(s.bias_made, 1)
    dve.wait_ge(s.consts_loaded, s.n_consts)
    dve.tensor_scalar(m.alog, m.alog, 84.0, None, ALU.min).then_inc(s.alog_held, 1)
    dve.wait_ge(s.a_exp, 1)
    dve.tensor_scalar(m.A[:, :, :], m.A[:, :, :], -1.0, None, ALU.mult).then_inc(s.bias_made, 1)


def setup_scalar(act, m, s):
    act.wait_ge(s.consts_loaded, s.n_consts)
    act.wait_ge(s.alog_held, 1)
    act.activation(m.A[:, :, :], m.alog, ACT.Exp).then_inc(s.a_exp, 1)
    act.wait_ge(s.wcomb_made, 1)
    act.activation(m.wcomb[:, :], m.bank[:, 0, :], ACT.Copy).then_inc(s.wcomb_copied, 1)


def setup_tensor(pe, m, s):
    pe.wait_ge(s.ident_made, 5)
    pe.wait_ge(s.latent_loaded, 11 * 16)
    for c in range(NC):
        mm = pe.matmul(m.bank[32 * c:32 * c + 32, 0, :], m.bd[:, c, :], m.wo_lat[:, c, :],
                       start=True, stop=True, tile_position=(0, 32 * c))
    mm.then_inc(s.wcomb_made, 1)
    pe.wait_ge(s.bvb_made, NC)
    for c in range(NC):
        mm = pe.matmul(m.bank[:, 1, :], m.bvb[:, c, :], m.wo_lat[:, c, :], start=(c == 0), stop=(c == NC - 1))
    mm.then_inc(s.latent_bias, 1)
    pe.wait_ge(s.bias_made, 2)
    pe.wait_ge(s.wcomb_copied, 1)



def build(nc, t, out):
    with ExitStack() as ctx:
        m = Memory(nc, ctx)

        def semaphore(name):
            return ctx.enter_context(nc.semaphore(name))

        def group():
            made = {}

            def sem(name):
                if name not in made:
                    made[name] = semaphore(name)
                return made[name]
            return made, sem

        engines = ("act", "dve", "pool", "pe")
        go = {e: semaphore("go_" + e) for e in engines}
        once, once_sem = group()
        each, each_sem = group()
        s = Signals(once_sem, each_sem)
        att, att_sem = group()
        feed, feed_sem = group()

        quarter = 1.0 / HD ** 0.5
        attA = Attention(att_sem, LN_A, True, quarter, HD,
                         lambda h: m.qA[:, h, :], lambda h: m.kA[:, h, :],
                         lambda h, kt: m.vA[:, kt, h, :], m.probsA, m.oA, m.ostA)
        attG = Attention(att_sem, LN_G, True, quarter, HD,
                         lambda h: m.qG[:, h, :], lambda h: m.kG[:, h // (H // KVH), :],
                         lambda h, kt: m.vG[:, kt, h // (H // KVH), :], m.probsG, m.oG, m.ostG, KVH)

        attM = Attention(att_sem, LN_M, False, 1.0 / LAT ** 0.5, LAT,
                         lambda h: m.qM[:, h // GRP, :], lambda h: m.kM[:, h % GRP, :],
                         lambda h, kt: m.vM[:, kt, :], m.probsM, m.oM, m.ostM)
        ff1 = Feed(feed_sem, LN_F1)
        ff2 = Feed(feed_sem, LN_F2)
        each_pass = [*each.values(), *att.values(), *feed.values()]

        wgq = m.wG[:, 0:2048].rearrange("p (c n) -> p c n", c=NC)
        wgkv = m.wG[:, 2048:3072].rearrange("p (c n) -> p c n", c=NC)
        wgo = m.wG[:, 3072:5120].rearrange("p (c n) -> p c n", c=NC)

        def rhs_a(w, c):
            return m.wA[:, w, c, :].rearrange("p (h d) -> p h d", d=HD)

        def rhs_g(w, c):
            return wgq[:, c, :].rearrange("p (h d) -> p h d", d=HD)

        rep_rows = nc.dram_tensor("state_rows", [2 * NS, S], F32).ap()
        x_mid = nc.dram_tensor("x_mid", [B, S, D], F32).ap()
        kv_mid = nc.dram_tensor("kv_mid", [2, KVH, B, S, HD], F32).ap()
        block = ctx.enter_context(nc.Block())

        def clear(sp, semaphores):
            numbers = sorted(x.num for x in semaphores)
            first = numbers[0]
            for x, after in zip(numbers, numbers[1:] + [None]):
                if after != x + 1:
                    sp.sem_clear(range(first, x + 1))
                    first = after

        def end_pass(sp, stored):
            sp.wait_ge(s.stored, stored)
            clear(sp, each_pass)
            for e in engines:
                sp.sem_inc(go[e], 1)

        def next_lap(sp, done, i):
            sp.wait_ge(s.x_updated, NT * (i + 1))
            clear(sp, done)
            sp.sem_inc(s.lap, 1)

        @block.sync
        def _(sp):
            setup_sync(sp, m, s, t)
            with sp.Fori(0, B) as b:
                sp.dma_start(m.x[:, :, :], t["x"][b].rearrange("(t p) d -> p t d", p=P)).then_inc(s.x_loaded, 16)
                for w, name in enumerate(("wq", "wk", "wv", "wo")):
                    sp.dma_start(m.wA[:, w], t[name].rearrange("(c p) n -> p c n", p=P)).then_inc(attA.w_loaded, 16)
                attend_sync(sp, m, attA, lambda hg, r: m.qA[96 + r:97 + r, GRP * hg:GRP * hg + GRP, :])
                sp.wait_ge(attA.valued, NT * NG)
                for z in range(2):
                    sp.dma_start(m.win[:, z], t["W_inT"][:, z * DI:(z + 1) * DI].rearrange("(c p) n -> p c n", p=P))\
                      .then_inc(s.win_loaded, 16)
                sp.dma_start(m.wx, t["W_xT"].rearrange("(m p) n -> p m n", p=P)).then_inc(s.wx_loaded, 16)
                sp.dma_start(m.wdt[0:RDT, :], t["W_dtT"]).then_inc(s.wx_loaded, 16)
                sp.dma_start(m.wout, t["W_outT"].rearrange("(m p) n -> p m n", p=P)).then_inc(s.wout_loaded, 16)
                next_lap(sp, att.values(), LN_A)
                attend_sync(sp, m, attM, lambda hg, r: m.qM[6 * LAT + r:6 * LAT + r + 97:32, hg, :])
                next_lap(sp, [*att.values(), *feed.values()], LN_M)
                scan_sync(sp, m, s, rep_rows)
                sp.wait_ge(s.y_made, NM)
                sp.dma_start(wgkv, t["Wkv_gqa"].rearrange("(c p) n -> p c n", p=P)).then_inc(s.wkv_loaded, 16)
                sp.wait_ge(s.x_updated, (LN_N1 + 1) * NT)
                sp.dma_start(x_mid[b].rearrange("(t p) d -> p t d", p=P), m.x[:, :, :]).then_inc(s.stored, 16)
                for tile in range(NT):
                    sp.wait_ge(s.kv_copied, tile + 1)
                    pairs = m.kvo[:, tile, :].rearrange("p (g z d) -> p g z d", g=KVH, z=2)
                    for z in range(2):
                        sp.dma_start(kv_mid[z, :, b, tile * P:(tile + 1) * P, :].rearrange("g p d -> p g d"),
                                     pairs[:, :, z, :]).then_inc(s.stored, 16)
                end_pass(sp, (1 + 2 * NT) * 16)
            sp.dma_start(wgq, t["Wq_gqa"].rearrange("(c p) n -> p c n", p=P)).then_inc(s.gqa_w_loaded, 16)
            sp.dma_start(wgo, t["Wo_gqa"].rearrange("(c p) n -> p c n", p=P)).then_inc(s.gqa_w_loaded, 16)
            with sp.Fori(0, B) as b:
                sp.dma_start(m.x[:, :, :], x_mid[b].rearrange("(t p) d -> p t d", p=P)).then_inc(s.x_loaded, 16)
                for tile in range(NT):
                    for z, to in enumerate((m.kt[:, tile, :].rearrange("p (g j d) -> p g j d", g=2, j=B),
                                            m.vG[:, tile, :, 0:HD].rearrange("p (g j) d -> p g j d", g=2))):
                        for g in range(2):
                            sp.dma_start(to[:, g], kv_mid[z, 2 * b + g, :, tile * P:(tile + 1) * P, :]
                                         .rearrange("j p d -> p j d")).then_inc(attG.kv_loaded, 16)
                attend_sync(sp, m, attG, lambda hg, r: m.qG[96 + r:97 + r, GRP * hg:GRP * hg + GRP, :])
                sp.wait_ge(s.x_updated, 2 * NT)
                sp.dma_start(out[b].rearrange("(t p) d -> p t d", p=P), m.x[:, :, :]).then_inc(s.stored, 16)
                end_pass(sp, 16)

        def next_pass(eng, name):
            eng.wait_ge(go[name], 1)
            eng.sem_clear(go[name])

        @block.gpsimd
        def _(pool):
            setup_gpsimd(pool, m, s)
            with pool.Fori(0, B):
                pool.wait_ge(s.nf4_ready, NC)
                ln_gpsimd(pool, m, s, LN_A)
                project_gpsimd(pool, m, s, attA, m.vA, m.tkA, H)
                ln_gpsimd(pool, m, s, LN_F1)
                add_bias_gpsimd(pool, m, s, LN_F1, 0, 0)
                pool.wait_ge(s.lap, 1)
                ln_gpsimd(pool, m, s, LN_M)
                add_bias_gpsimd(pool, m, s, LN_M, 1, 1)
                latent_gpsimd(pool, m, s, attM)
                pool.wait_ge(s.lap, 2)
                ln_gpsimd(pool, m, s, LN_F2)
                add_bias_gpsimd(pool, m, s, LN_F2, 2, 0)
                ln_gpsimd(pool, m, s, LN_S)
                scan_gpsimd(pool, m, s)
                ln_gpsimd(pool, m, s, LN_N1)
                add_bias_gpsimd(pool, m, s, LN_N1, 3, 2)
                ln_gpsimd(pool, m, s, LN_KV)
                next_pass(pool, "pool")
            with pool.Fori(0, B):
                ln_gpsimd(pool, m, s, LN_G)
                project_gpsimd(pool, m, s, attG, m.vG, m.tkG, KVH)
                add_bias_gpsimd(pool, m, s, LN_G, 0, 3)
                ln_gpsimd(pool, m, s, LN_N2)
                add_bias_gpsimd(pool, m, s, LN_N2, 1, 2)
                next_pass(pool, "pool")

        @block.scalar
        def _(act):
            setup_scalar(act, m, s)
            with act.Fori(0, B):
                ln_scalar(act, m, s, LN_A)
                project_scalar(act, m, s, attA, H, m.rqA, m.rrA, m.tqA, m.tkA, m.vA, m.qA, m.kA)
                attend_scalar(act, m, attA)
                output_scalar(act, m, attA)
                ln_scalar(act, m, s, LN_F1)
                feed_scalar(act, m, s, ff1)
                act.wait_ge(s.lap, 1)
                ln_scalar(act, m, s, LN_M)
                latent_scalar(act, m, s, attM)
                attend_scalar(act, m, attM)
                latent_output_scalar(act, m, attM)
                act.wait_ge(s.lap, 2)
                ln_scalar(act, m, s, LN_F2)
                feed_scalar(act, m, s, ff2)
                ln_scalar(act, m, s, LN_S)
                scan_scalar(act, m, s)
                ln_scalar(act, m, s, LN_N1)
                ln_scalar(act, m, s, LN_KV)
                kv_scalar(act, m, s)
                next_pass(act, "act")
            with act.Fori(0, B):
                ln_scalar(act, m, s, LN_G)
                project_scalar(act, m, s, attG, KVH, m.rqG, m.rrG, m.tqG, m.tkG, m.vG, m.qG, m.kG)
                attend_scalar(act, m, attG)
                output_scalar(act, m, attG)
                ln_scalar(act, m, s, LN_N2)
                next_pass(act, "act")

        @block.vector
        def _(dve):
            setup_vector(dve, m, s)
            with dve.Fori(0, B):
                ln_vector(dve, m, s, LN_A)
                project_vector(dve, m, s, attA, H, m.rqA, m.rrA, m.tqA, m.tkA, m.qA, m.kA)
                attend_vector(dve, m, attA)
                residual_vector(dve, m, s, LN_A, attA.out_made, lambda t: t % 2)
                ln_vector(dve, m, s, LN_F1)
                feed_vector(dve, m, s, ff1)
                residual_vector(dve, m, s, LN_F1, ff1.out_made, lambda t: 6 + t % 2, 0)
                dve.wait_ge(s.lap, 1)
                ln_vector(dve, m, s, LN_M)
                latent_vector(dve, m, s, attM)
                attend_vector(dve, m, attM)
                residual_vector(dve, m, s, LN_M, attM.out_made, lambda t: t % 2, 1)
                dve.wait_ge(s.lap, 2)
                ln_vector(dve, m, s, LN_F2)
                feed_vector(dve, m, s, ff2)
                residual_vector(dve, m, s, LN_F2, ff2.out_made, lambda t: 6 + t % 2, 2)
                ln_vector(dve, m, s, LN_S)
                scan_vector(dve, m, s)
                residual_vector(dve, m, s, LN_S, s.scan_out_made, lambda t: 2 + t)
                ln_vector(dve, m, s, LN_N1)
                residual_vector(dve, m, s, LN_N1, s.n1_made, lambda t: t, 3)
                ln_vector(dve, m, s, LN_KV)
                next_pass(dve, "dve")
            with dve.Fori(0, B):
                ln_vector(dve, m, s, LN_G)
                project_vector(dve, m, s, attG, KVH, m.rqG, m.rrG, m.tqG, m.tkG, m.qG, m.kG)
                attend_vector(dve, m, attG)
                residual_vector(dve, m, s, LN_G, attG.out_made, lambda t: t % 2, 0)
                ln_vector(dve, m, s, LN_N2)
                residual_vector(dve, m, s, LN_N2, s.n2_made, lambda t: t, 1)
                next_pass(dve, "dve")

        @block.tensor
        def _(pe):
            setup_tensor(pe, m, s)

            def stacks_ready(a, kv_heads):
                n = len(lots(kv_heads))

                def wait(pe):
                    pe.wait_ge(a.placed_dve, (n + 1) // 2)
                    pe.wait_ge(a.placed_act, n // 2)
                    pe.wait_ge(*((a.v_read, NT) if a.rope else (a.kv_loaded, 64 * NT)))
                return wait

            def latent_ready(pe):
                pe.wait_ge(attM.placed_dve, NT)
                pe.wait_ge(s.klat_placed, GRP)
                pe.wait_ge(s.vlat_made, 1)

            with pe.Fori(0, B):
                ln_tensor(pe, m, s, LN_A)
                project_tensor(pe, m, s, attA, H, rhs_a, lambda pe, w: pe.wait_ge(attA.w_loaded, 64),
                               m.tqA, m.tkA)
                attend_tensor(pe, m, attA, stacks_ready(attA, H))
                output_tensor(pe, m, s, attA, m.wA[:, 3], lambda pe: None)
                ln_tensor(pe, m, s, LN_F1)
                feed_tensor(pe, m, s, ff1)
                pe.wait_ge(s.lap, 1)
                ln_tensor(pe, m, s, LN_M)
                latent_tensor(pe, m, s, attM)
                attend_tensor(pe, m, attM, latent_ready)
                latent_output_tensor(pe, m, s, attM)
                pe.wait_ge(s.lap, 2)
                ln_tensor(pe, m, s, LN_F2)
                feed_tensor(pe, m, s, ff2)
                ln_tensor(pe, m, s, LN_S)
                scan_tensor(pe, m, s)
                ln_tensor(pe, m, s, LN_N1)
                nf4_tensor(pe, m, s, LN_N1, s.n1_made)
                ln_tensor(pe, m, s, LN_KV)
                kv_tensor(pe, m, s, wgkv)
                next_pass(pe, "pe")
            with pe.Fori(0, B):
                ln_tensor(pe, m, s, LN_G)
                project_tensor(pe, m, s, attG, KVH, rhs_g, lambda pe, w: pe.wait_ge(s.gqa_w_loaded, 32),
                               m.tqG, m.tkG)
                attend_tensor(pe, m, attG, stacks_ready(attG, KVH))
                output_tensor(pe, m, s, attG, wgo, lambda pe: None)
                ln_tensor(pe, m, s, LN_N2)
                nf4_tensor(pe, m, s, LN_N2, s.n2_made)
                next_pass(pe, "pe")


def kernel(**inputs):
    import numpy as np
    import concourse.bacc as bacc
    from concourse.bass_utils import run_bass_kernel_spmd

    def tiles(x):
        return x.reshape(-1, P).T

    inv = 1.0 / 10000.0 ** (np.arange(0, HD, 2)[:HD // 2].astype(np.float32) / HD)
    angle = np.outer(np.arange(S), inv).astype(np.float32)
    cos = np.repeat(np.cos(angle), 2, axis=1)
    sin = np.stack((-np.sin(angle), np.sin(angle)), axis=-1).reshape(S, HD)

    b1 = np.zeros((2, NF * P), np.float32)
    b1[:, :INTER] = np.asarray(inputs["L0_ffn_b1"]).reshape(2, INTER)
    g = {k: np.asarray(v) for k, v in inputs.items()}
    arrays = {
        "x": g["L0_attn_a_x"], "wq": g["L0_attn_a_wq"], "wk": g["L0_attn_a_wk"], "wv": g["L0_attn_a_wv"],
        "wo": g["L0_attn_a_wo"], "Wq_d": g["L0_attn_b_Wq_d"], "bq_d": g["L0_attn_b_bq_d"],
        "W_qk": g["L0_attn_b_W_qk"], "b_qk": g["L0_attn_b_b_qk"], "Wkv_d": g["L0_attn_b_Wkv_d"],
        "bkv_d": g["L0_attn_b_bkv_d"], "Wv_uT": g["L0_attn_b_Wv_u"].T, "bv": tiles(g["L0_attn_b_bv_u"]),
        "Wo_lat": g["L0_attn_b_Wo"], "bo_lat": g["L0_attn_b_bo"], "U1": g["L0_ffn_U1"],
        "V1": g["L0_ffn_V1"], "U2": g["L0_ffn_U2"], "V2": g["L0_ffn_V2"],
        "b1": b1.reshape(2, NF, P).transpose(2, 0, 1), "b2": g["L0_ffn_b2"],
        "W_inT": g["L1_attn_a_W_in"].T, "conv_w": g["L1_attn_a_conv_w"],
        "conv_b": tiles(g["L1_attn_a_conv_b"]), "W_xT": g["L1_attn_a_W_x"].T,
        "W_dtT": g["L1_attn_a_W_dt"].T, "b_dt": tiles(g["L1_attn_a_b_dt"]),
        "A_log": g["L1_attn_a_A_log"], "D": tiles(g["L1_attn_a_D"]), "W_outT": g["L1_attn_a_W_out"].T,
        "Wq_gqa": g["L1_attn_b_Wq"], "Wkv_gqa": g["L1_attn_b_Wkv"], "Wo_gqa": g["L1_attn_b_Wo"],
        "bo_gqa": g["L1_attn_b_bo"], "codesT": g["L1_ffn_codes"].T,
        "absmaxT": g["L1_ffn_absmax"].reshape(D, D // 64).T, "bias_nf4": g["L1_ffn_bias"],
        "cos": cos, "sin": sin,
    }
    arrays = {k: np.ascontiguousarray(v) for k, v in arrays.items()}
    nc = bacc.Bacc("TRN2", target_bir_lowering=False, num_devices=1)
    t = {k: nc.dram_tensor(f"in_{k}", v.shape, mybir.dt.from_np(v.dtype), kind="ExternalInput").ap()
         for k, v in arrays.items()}
    out = nc.dram_tensor("out", (B, S, D), F32, kind="ExternalOutput").ap()
    build(nc, t, out)
    r = run_bass_kernel_spmd(nc, [{f"in_{k}": v for k, v in arrays.items()}], core_ids=[0])
    return r.results[0]["out"]
```
